# Optimizing a Trainium2 kernel written in Bass

```python
import numpy as np
import jax
import jax.numpy as jnp

def _softmax(x, axis=-1):
    return jax.nn.softmax(x, axis=axis)

def _gelu(x):
    return jax.nn.gelu(x, approximate=True)

def _silu(x):
    return jax.nn.silu(x)

def _sigmoid(x):
    return jax.nn.sigmoid(x)

def _layernorm(x, axis=-1, eps=1e-05):
    m = jnp.mean(x, axis=axis, keepdims=True)
    v = jnp.var(x, axis=axis, keepdims=True)
    return (x - m) / jnp.sqrt(v + eps)

def _scatter_add(tgt, idx, src, axis=0):
    return tgt.at[idx].add(src)

def _segment_sum(src, seg, n):
    return jax.ops.segment_sum(src, seg, n)
kernel_name = 'mk_adj_resnorm_d4_adj_r2_98d737'

def setup_inputs(seed: int=0):
    np.random.seed(seed)
    _w = jnp.asarray

    def _rec_inputs():
        import jax
        import jax.numpy as jnp
        _gk = jax.random.key(seed)
        x = -0.0005207 + 1.001 * jax.random.normal(jax.random.fold_in(_gk, 1), (16, 512, 64), jnp.float32)
        _a = jax.random.bernoulli(jax.random.fold_in(_gk, 2), 0.0078125, (512, 512))
        _a = jnp.logical_or(_a, jnp.swapaxes(_a, -1, -2))
        _a = jnp.logical_or(_a, jnp.eye(512, dtype=bool))
        _af = _a.astype(jnp.float32)
        _af = _af * jax.random.uniform(jax.random.fold_in(_gk, 3), (512, 512), jnp.float32, 0.05, 5.41998)
        adj = _af
        return (x, adj)
    x, adj = _rec_inputs()

    def _L0_gnn_setup():
        import jax, jax.numpy as jnp
        import numpy as np
        B, N, F, L = (4, 4096, 64, 2)
        key = jax.random.key(seed)
        k1, k2, k3 = jax.random.split(key, 3)
        x = jax.random.normal(k1, (B, N, F), dtype=jnp.float32)
        net_params = jax.random.normal(k2, (L * F * F,), dtype=jnp.float32)
        A = jax.random.normal(k3, (N, N), dtype=jnp.float32)
        return {'x': x, 't': 0, 'net_params': net_params, 'A': A}
    _L0_gnn_all = _L0_gnn_setup()
    _L0_gnn_in = {k: v for k, v in _L0_gnn_all.items() if k in ('net_params',)}
    del _L0_gnn_all

    def _L1_gnn_setup():
        import jax, jax.numpy as jnp
        import numpy as np
        NEG_INF = -1e+16

        def gat_layer(x, graph, W, b):
            h = x @ W
            s = jnp.einsum('bnd,bmd->bnm', h, h) * graph
            s = jnp.where(s == 0.0, NEG_INF, s)
            a = jax.nn.softmax(s, axis=2)
            return jnp.einsum('bnm,bmd->bnd', a, h) + b
        key = jax.random.key(seed)
        k1, k2, k3, k4, k5, k6 = jax.random.split(key, 6)
        B, N, C_IN, HID, HEADS, C_OUT = (16, 512, 64, 128, 8, 64)
        flow_x = jax.random.normal(k1, (B, N, C_IN), dtype=jnp.float32)
        graph = jax.random.randint(k2, (N, N), 0, 2).astype(jnp.float32)
        Wh = jax.random.normal(k3, (HEADS, C_IN, HID), dtype=jnp.float32)
        bh = jax.random.normal(k4, (HEADS, HID), dtype=jnp.float32)
        W_out = jax.random.normal(k5, (HID * HEADS, C_OUT), dtype=jnp.float32)
        b_out = jax.random.normal(k6, (C_OUT,), dtype=jnp.float32)
        return {'flow_x': flow_x, 'graph': graph, 'Wh': Wh, 'bh': bh, 'W_out': W_out, 'b_out': b_out}
    _L1_gnn_all = _L1_gnn_setup()
    _L1_gnn_in = {k: v for k, v in _L1_gnn_all.items() if k in ('Wh', 'bh', 'W_out', 'b_out')}
    del _L1_gnn_all

    def _L2_gnn_setup():
        import jax, jax.numpy as jnp
        import numpy as np
        B, N, IN_SIZE, K, OUT = (32, 1024, 64, 2, 64)
        NUM_MATRICES = 2 * K + 1
        key = jax.random.key(seed)
        k1, k2, k3, k4 = jax.random.split(key, 4)
        inputs_and_state = jax.random.normal(k1, (B, N, IN_SIZE), dtype=jnp.float32)
        support0 = jax.random.uniform(k2, (N, N), dtype=jnp.float32) / N
        support1 = jax.random.uniform(k3, (N, N), dtype=jnp.float32) / N
        fan_in, fan_out = (IN_SIZE * NUM_MATRICES, OUT)
        std = 1.414 * np.sqrt(2.0 / (fan_in + fan_out))
        weight = jax.random.normal(k4, (fan_in, fan_out), dtype=jnp.float32) * std
        bias = jnp.zeros((OUT,), dtype=jnp.float32)
        return {'inputs_and_state': inputs_and_state, 'support0': support0, 'support1': support1, 'weight': weight, 'bias': bias}
    _L2_gnn_all = _L2_gnn_setup()
    _L2_gnn_in = {k: v for k, v in _L2_gnn_all.items() if k in ('weight', 'bias')}
    del _L2_gnn_all

    def _L3_gnn_setup():
        import jax, jax.numpy as jnp
        import numpy as np
        B, N, F_IN, F_OUT = (32768, 17, 64, 64)
        key = jax.random.key(seed)
        k1, k2, k3, k4 = jax.random.split(key, 4)
        x = jax.random.normal(k1, (B, N, F_IN), dtype=jnp.float32)
        adj = jax.random.uniform(k2, (N, N), dtype=jnp.float32)
        adj = (adj + adj.T) * 0.5
        weight_self = jax.random.normal(k3, (F_IN, F_OUT), dtype=jnp.float32) * (1.0 / np.sqrt(F_IN))
        weight_neighbor = jax.random.normal(k4, (F_IN, F_OUT), dtype=jnp.float32) * (1.0 / np.sqrt(F_IN))
        bias = jnp.zeros((F_OUT,), dtype=jnp.float32)
        return {'x': x, 'adj': adj, 'weight_self': weight_self, 'weight_neighbor': weight_neighbor, 'bias': bias}
    _L3_gnn_all = _L3_gnn_setup()
    _L3_gnn_in = {k: v for k, v in _L3_gnn_all.items() if k in ('weight_self', 'weight_neighbor', 'bias')}
    del _L3_gnn_all
    return {'x': x, 'adj': adj, 'L0_gnn_net_params': _L0_gnn_in['net_params'], 'L1_gnn_Wh': _L1_gnn_in['Wh'], 'L1_gnn_bh': _L1_gnn_in['bh'], 'L1_gnn_W_out': _L1_gnn_in['W_out'], 'L1_gnn_b_out': _L1_gnn_in['b_out'], 'L2_gnn_weight': _L2_gnn_in['weight'], 'L2_gnn_bias': _L2_gnn_in['bias'], 'L3_gnn_weight_self': _L3_gnn_in['weight_self'], 'L3_gnn_weight_neighbor': _L3_gnn_in['weight_neighbor'], 'L3_gnn_bias': _L3_gnn_in['bias']}

def reference(x, adj, L0_gnn_net_params, L1_gnn_Wh, L1_gnn_bh, L1_gnn_W_out, L1_gnn_b_out, L2_gnn_weight, L2_gnn_bias, L3_gnn_weight_self, L3_gnn_weight_neighbor, L3_gnn_bias):
    import jax
    import jax.numpy as jnp

    def _L0_gnn_ref(x, t, net_params, A):
        import jax, jax.numpy as jnp
        import numpy as np
        B, N, F, L = (4, 4096, 64, 2)
        weights = net_params.reshape(L, F, F)
        z = x.reshape(-1, A.shape[1], F)
        for i in range(L):
            h = jnp.einsum('mn,bnf->bmf', A, z)
            z = jnp.einsum('bmf,fg->bmg', h, weights[i])
            z = jax.nn.relu(z)
        return z

    def _L1_gnn_ref(flow_x, graph, Wh, bh, W_out, b_out):
        import jax, jax.numpy as jnp
        import numpy as np
        NEG_INF = -1e+16

        def gat_layer(x, graph, W, b):
            h = x @ W
            s = jnp.einsum('bnd,bmd->bnm', h, h) * graph
            s = jnp.where(s == 0.0, NEG_INF, s)
            a = jax.nn.softmax(s, axis=2)
            return jnp.einsum('bnm,bmd->bnd', a, h) + b
        heads = jax.vmap(lambda W, b: gat_layer(flow_x, graph, W, b))(Wh, bh)
        H, B, N, D = heads.shape
        cat = jnp.moveaxis(heads, 0, 2).reshape(B, N, H * D)
        x = jax.nn.leaky_relu(cat, negative_slope=0.01)
        out = gat_layer(x, graph, W_out, b_out)
        return jax.nn.leaky_relu(out, negative_slope=0.01)

    def _L2_gnn_ref(inputs_and_state, support0, support1, weight, bias):
        import jax, jax.numpy as jnp
        import numpy as np
        B, N, IN_SIZE, K, OUT = (32, 1024, 64, 2, 64)
        NUM_MATRICES = 2 * K + 1
        x0 = inputs_and_state
        x_stack = [x0]
        for support in (support0, support1):
            x1 = jnp.einsum('ij,bjk->bik', support, x0)
            x_stack.append(x1)
            x_prev, x_curr = (x0, x1)
            for _ in range(2, K + 1):
                x2 = 2.0 * jnp.einsum('ij,bjk->bik', support, x_curr) - x_prev
                x_stack.append(x2)
                x_prev, x_curr = (x_curr, x2)
        x_cat = jnp.concatenate(x_stack, axis=-1)
        out = jnp.einsum('bnf,fo->bno', x_cat, weight) + bias
        return out

    def _L3_gnn_ref(x, adj, weight_self, weight_neighbor, bias):
        import jax, jax.numpy as jnp
        import numpy as np
        B, N, F_IN, F_OUT = (32768, 17, 64, 64)
        out_self = jnp.einsum('bni,io->bno', x, weight_self)
        x_neighbors = jnp.einsum('nm,bmi->bni', adj, x)
        out_neighbors = jnp.einsum('bni,io->bno', x_neighbors, weight_neighbor)
        return out_self + out_neighbors + bias
    x = _layernorm(x + _L0_gnn_ref(x, 0, L0_gnn_net_params, adj), axis=-1)
    x = _layernorm(x + _L1_gnn_ref(x, adj, L1_gnn_Wh, L1_gnn_bh, L1_gnn_W_out, L1_gnn_b_out), axis=-1)
    x = _layernorm(x + _L2_gnn_ref(x, adj, adj, L2_gnn_weight, L2_gnn_bias), axis=-1)
    x = _layernorm(x + _L3_gnn_ref(x, adj, L3_gnn_weight_self, L3_gnn_weight_neighbor, L3_gnn_bias), axis=-1)
    return x

_drawn_inputs = setup_inputs


def setup_inputs(seed=0):
    import zlib

    import numpy as np

    out = dict(_drawn_inputs(seed))
    spreads = {'L2_gnn_bias': (0.0, 0.8), 'L3_gnn_bias': (0.0, 0.8)}
    factors = {'L1_gnn_b_out': 8.0}
    for name, (base, spread) in spreads.items():
        noise = np.random.default_rng([zlib.crc32(name.encode()), seed]).standard_normal(out[name].shape)
        drawn = base * np.exp(spread * noise) if base else spread * noise
        out[name] = jnp.asarray(drawn.astype(out[name].dtype))
    for name, factor in factors.items():
        out[name] = (out[name] * factor).astype(out[name].dtype)
    return out
```

```python
from contextlib import ExitStack

import concourse.bass as bass
from concourse import mybir

ALU = mybir.AluOpType
ACT = mybir.ActivationFunctionType
F32 = mybir.dt.float32
F16 = mybir.dt.float16
BF16 = mybir.dt.bfloat16
AX = mybir.AxisListType.X

P = 128
B = 16
N = 512
F = 64
NB = N // P
H = 8
D = 128
PAIRS = B // 2
COLS = B * F
EPS = 1e-5
SLOPE = 0.01
NEG = -1e16
S_SCALE = 2.0 ** -6
P_SCALE = 2.0 ** 4
H_SCALE = 2.0 ** -3
Q_SCALE = 2.0 ** -4

ARENA = 39936
SEMAPHORES = """
    ld_adj ld_x ld_w ld_b stored
    zeroed consts bd_sum bd_ready wo wd adjx
    at_ps at_hi at_lo wt_ps wt_sb g_ps g_hi g_lo
    xt_ps xt_sb proj_ps q_hi q_done f_done am_ps am_ev xb q1_hi q1_lo
    r_ready mean_sum mean_neg cen sq var_sum var_eps sd rs x_ready
    xd xvh xvl pt_ps u_hi u_lo h2_hi xhh xll
    y_ps y_hi y_lo s_ps s_max s_neg s_exp s_rec s_norm t_ps p_hi p_lo
    av_ps u_sb o_ps bhs c_small c_sb c_hi c_lo h2_ps h2_sb
    pm_cols pm_rows xh2 xl2 xv2h xv2l no_ps g2 lr
"""

LAG = {
    "scores": 11.2, "turn_probs": 17.7,
    "left_proj": 9.4, "times_values": 23.3, "head_out": 25.6, "add_h2": 31.8,
    "columns": 4.1,
    "exps": 15.0, "probs_high": 17.9,
    "left_high": 9.2, "u_high": 23.4, "cat_small": 25.4, "cat_high": 26.9,
    "twice": 2.7, "columns_high": 4.4, "keep_high": 32.1,
    "scale_max": 12.0, "recip": 16.95, "probs_low": 18.9,
    "left_low": 10.3, "u_low": 24.3, "cat": 26.8,
    "columns_low": 5.4, "keep_low": 35.3,
    "negate": 11.3, "norm": 15.9,
    "cat_low": 27.4, "values_high": 5.8, "values_low": 5.9,
    "sum_h2": 9.1, "sum_h2_rows": 11.1, "rows_out": 25.6,
    "h2_high": 9.7, "h2_rows_high": 12.1,
    "h2_low": 10.0, "h2_rows_low": 12.2, "take_u": 24.3, "take_out": 26.8,
}
TAIL = 40
T_RING = 8
P_RING = 8
V_RING = 8
HEAD_SLOTS = NB * H
TILES = NB * B * (H + 1)
RECIP_AHEAD = 5


def build(nc, x, adj, net, wh, bh, w_out, b_out, w2, b2, w_self, w_nb, b3, out):
    with ExitStack() as ctx:
        def sb(name, shape, dt):
            return ctx.enter_context(nc.sbuf_tensor(name, shape, dt))

        X = sb("X", [P, NB, COLS], F32)
        ADJX = sb("ADJX", [P, NB, N], F32)
        MASK = sb("MASK", [P, NB, N], BF16)
        ATh = sb("ATh", [P, NB, N], F16)
        ATl = sb("ATl", [P, NB, N], F16)
        BD = sb("BD", [P, 7, P], F32)
        ident = sb("ident", [P, P], F32)
        identb = sb("identb", [P, P], BF16)
        IIh = sb("IIh", [P, P], F16)
        II = sb("II", [P, P], F32)
        IIs = sb("IIs", [P, F], F32)
        bout = sb("bout", [P, F], F32)
        bias2 = sb("bias2", [P, F], F32)
        bias3 = sb("bias3", [P, F], F32)
        bhT = sb("bhT", [P, H], F32)
        bhP = sb("bhP", [P, H], F32)
        bhS = sb("bhS", [P, H], F32)
        GS = sb("GS", [P, H, P], F16)
        Wa = sb("Wa", [P, H, D], F16)
        Wb = sb("Wb", [P, H, D], F16)
        WO = sb("WO", [P, H, P], F16)
        stat = sb("stat", [P, 2, 8, B], F32)
        zero = sb("zero", [P, 1], F32)
        mx = sb("mx", [P, V_RING], F32)
        negm = sb("negm", [P, V_RING], F32)
        rsum = sb("rsum", [P, V_RING], F32)
        rinv = sb("rinv", [P, V_RING], F32)

        arena = sb("arena", [P, ARENA], F32)
        top = [0]

        def part(words, dt=F32):
            a = arena[:, top[0]:top[0] + words]
            top[0] += words
            assert top[0] <= ARENA, top[0]
            return a if dt == F32 else a.bitcast(dt)

        ADJ = part(NB * N).rearrange("p (i m) -> p i m", i=NB)
        WRAW = part(9 * F).rearrange("p (k f) -> p k f", k=9)
        WH2 = part(H * D).rearrange("p (h d) -> p h d", h=H)
        WT = part(H * P).rearrange("p (h d) -> p h d", h=H)
        WOR = part(H * F).rearrange("p (h d) -> p h d", h=H)
        tmpw = part(2 * F).rearrange("p (k f) -> p k f", k=2)
        Qh = part(NB * COLS, F16).rearrange("p (s j c) -> p s j c", s=2, j=NB)
        Ql = part(NB * COLS, F16).rearrange("p (s j c) -> p s j c", s=2, j=NB)
        XT = part(2 * N).rearrange("p (e n) -> p e n", e=2)
        Z = part(NB * COLS).rearrange("p (i c) -> p i c", i=NB)
        F1 = Z
        XB = part(NB * COLS).rearrange("p (i c) -> p i c", i=NB)
        EV = part(2 * COLS).rearrange("p (e c) -> p e c", e=2)
        R = part(2 * COLS).rearrange("p (e c) -> p e c", e=2)
        CEN = part(2 * COLS).rearrange("p (e c) -> p e c", e=2)
        SQ = part(COLS)
        top[0] = 0
        XHH = part(B * N // 2, F16).rearrange("p (b n) -> p b n", b=B)
        G2 = arena[:, 0:NB * COLS].rearrange("p (i c) -> p i c", i=NB)
        XLL = part(B * N // 2, F16).rearrange("p (b n) -> p b n", b=B)
        XV = part(B * N // 2, F16).rearrange("p (b j c) -> p b j c", b=B, j=NB)
        PH = part(N * NB, F16).rearrange("p (e j n) -> p e j n", e=2, j=NB)
        PL = part(N * NB, F16).rearrange("p (e j n) -> p e j n", e=2, j=NB)
        H2h = part(B * N // 2, F16).rearrange("p (b n) -> p b n", b=B)
        H2l = part(B * N // 2, F16).rearrange("p (b n) -> p b n", b=B)
        PR = part(P_RING * N).rearrange("p (r m) -> p r m", r=P_RING)
        TS = part(T_RING * N).rearrange("p (r m) -> p r m", r=T_RING)
        US = part(2 * N).rearrange("p (e n) -> p e n", e=2)
        UA = part(N, F16).rearrange("p (e n) -> p e n", e=2)
        UB = part(N, F16).rearrange("p (e n) -> p e n", e=2)
        CS = part(N)
        C32 = part(2 * N).rearrange("p (e n) -> p e n", e=2)
        CH = part(N, F16).rearrange("p (e n) -> p e n", e=2)
        CL = part(N, F16).rearrange("p (e n) -> p e n", e=2)
        YS = part(N, F16).rearrange("p (e n) -> p e n", e=2)
        XD = part(N).rearrange("p (i t f) -> p i t f", i=NB, t=2)
        XHH2 = part(N, F16).rearrange("p (e n) -> p e n", e=2)
        XLL2 = part(N, F16).rearrange("p (e n) -> p e n", e=2)

        PS = ctx.enter_context(nc.psum_tensor("PS", [P, 8, N], F32))
        bS = [PS[:, 0, :], PS[:, 1, :]]
        bT = [PS[:, 2, :], PS[:, 3, :]]
        bU, bO, bH, bY = PS[:, 4, :], PS[:, 5, :], PS[:, 6, :], PS[:, 7, :]

        S = {name: ctx.enter_context(nc.semaphore(name)) for name in SEMAPHORES.split()}

        def wait(eng, name, value):
            if isinstance(value, int) and value <= 0:
                return
            eng.wait_ge(S[name], value)
            if eng is nc.gpsimd and not isinstance(value, int):
                eng.nop(nofuse=True)

        def wait_at_ends(eng, name, value):
            if isinstance(value, int):
                wait(eng, name, value)

        block = ctx.enter_context(nc.Block())

        class At:
            def __init__(self, phase, it):
                self.heads = phase == "heads"
                self.it = it
                self.base = HEAD_SLOTS * it if self.heads else 2 * NB * it + HEAD_SLOTS * B
                self.ubase = H * it if self.heads else 2 * it + H * B

            def graph(self, u):
                return self.it + u // H if self.heads else 2 * self.it + u

        def slot(s, bodies):
            turns = []
            for n, (at, tile_ops, unit_ops, low, high) in enumerate(bodies):
                for ops, every in ((tile_ops, 1), (unit_ops, NB)):
                    for op, name in ops:
                        first = s - int(LAG[name])
                        if first % every == 0 and low <= first < high:
                            turns.append((LAG[name] % 1, n, len(turns), op, at, first // every))
            for *_, op, at, index in sorted(turns, key=lambda t: t[:3]):
                op(at, index)

        def attention(eng, tile_ops, head_ops, out_ops):
            far = 1 << 20
            for s in range(HEAD_SLOTS):
                slot(s, [(At("heads", 0), tile_ops, head_ops, 0, far)])
            with eng.Fori(1, B) as it:
                for s in range(HEAD_SLOTS):
                    slot(s, [(At("heads", it), tile_ops, head_ops, -far, far)])
            for s in range(TAIL):
                slot(s, [(At("heads", B), tile_ops, head_ops, -far, 0),
                         (At("out", 0), tile_ops, out_ops, 0, far)])
            with eng.Fori(TAIL // (2 * NB), B // 2) as it:
                for s in range(2 * NB):
                    slot(s, [(At("out", it), tile_ops, out_ops, -far, far)])
            for s in range(TAIL):
                slot(s, [(At("out", B // 2), tile_ops, out_ops, -far, 0)])

        @block.sync
        def _(sp):
            sp.dma_start(ADJ, adj.rearrange("(i p) m -> p i m", p=P)).then_inc(S["ld_adj"], 16)
            for i in range(NB):
                sp.dma_start(X[:, i, :].rearrange("p (b f) -> p b f", b=B),
                             x.rearrange("b (i p) f -> i p b f", p=P)[i]).then_inc(S["ld_x"], 16)
            for half in (0, 1):
                rows = slice(F * half, F * half + F)
                sp.dma_start(WRAW[rows, 0:2, :], net.rearrange("(l f g) -> f l g", f=F, g=F)).then_inc(S["ld_w"], 16)
                sp.dma_start(WRAW[rows, 2:7, :], w2.rearrange("(k f) o -> f k o", f=F)).then_inc(S["ld_w"], 16)
                sp.dma_start(WRAW[rows, 7, :], w_self).then_inc(S["ld_w"], 16)
                sp.dma_start(WRAW[rows, 8, :], w_nb).then_inc(S["ld_w"], 16)
                sp.dma_start(WH2[rows, :, :], wh.rearrange("h c d -> c h d")).then_inc(S["ld_w"], 16)
            sp.dma_start(WOR, w_out.rearrange("(h d) o -> d h o", d=D)).then_inc(S["ld_w"], 16)
            sp.dma_start(bhT[:, :], bh.rearrange("h d -> d h"), allow_slow_non_contiguous=True).then_inc(S["ld_b"], 16)
            for dst, src in ((bout, b_out), (bias2, b2), (bias3, b3)):
                sp.dma_start(dst[:, :], src.rearrange("(a f) -> a f", a=1).broadcast_to([P, F])).then_inc(S["ld_b"], 16)
            for i in range(NB):
                sp.wait_ge(S["x_ready"], 3 * NB + i + 1)
                sp.dma_start(out.rearrange("b (i p) f -> i p b f", p=P)[i],
                             X[:, i, :].rearrange("p (b f) -> p b f", b=B)).then_inc(S["stored"], 16)
            sp.wait_ge(S["stored"], 16 * NB)

        LD_W = 11 * 16
        LD_B = 4 * 16
        PROJ = [[0], [1], [2, 3, 4], [6, 5]]
        FB = [[6, 7], [0, 1]]
        A_OF_P = [0, 1, 2, 4]
        QSET = [0, 1, 0, 1, 0]
        HALF = COLS // 2

        def cols(p):
            return slice(P * p, P * p + P)

        def halfc(c):
            return slice(HALF * c, HALF * c + HALF)

        def blocks(bank):
            return PS[:, bank, :].rearrange("p (i c) -> p i c", i=NB)

        def groups(ap):
            return ap.rearrange("p (b f) -> p b f", b=B)

        @block.gpsimd
        def _(pool):
            pool.memset(ident[:, :], 0.0).then_inc(S["zeroed"], 1)
            pool.memset(II[:, :], 0.0).then_inc(S["zeroed"], 1)
            pool.memset(zero[:, :], 0.0).then_inc(S["consts"], 1)
            pool.memset(BD[:, :, :], 0.0).then_inc(S["zeroed"], 1)
            pool.wait_ge(S["zeroed"], 3)
            pool.affine_select(out=ident[:, :], in_=ident[:, :], compare_op=ALU.not_equal, fill=1.0,
                               base=0, pattern=[[-1, P]], channel_multiplier=1).then_inc(S["consts"], 1)
            for k, base in enumerate((0, F, -F)):
                pool.wait_ge(S["consts"], 2 + k)
                pool.affine_select(out=II[:, :], in_=II[:, :], compare_op=ALU.not_equal, fill=1.0,
                                   base=base, pattern=[[-1, P]], channel_multiplier=1).then_inc(S["consts"], 1)
            pool.wait_ge(S["consts"], 5)
            pool.tensor_copy(identb[:, :], ident[:, :]).then_inc(S["consts"], 1)
            pool.tensor_copy(IIh[:, :], II[:, :]).then_inc(S["consts"], 1)
            pool.tensor_scalar(IIs[:, :], II[:, 0:F], 1.0 / (P_SCALE * H_SCALE), None, ALU.mult).then_inc(S["consts"], 1)
            pool.wait_ge(S["ld_w"], LD_W)
            pool.tensor_copy(WO[:, :, 0:F], WOR).then_inc(S["wo"], 1)
            pool.wait_ge(S["wo"], 1)
            pool.tensor_tensor(WO[:, :, F:P], WOR, WO[:, :, 0:F], ALU.subtract).then_inc(S["wo"], 1)
            pool.tensor_copy(Wa[:, :, :], WH2).then_inc(S["wd"], 1)
            pool.tensor_copy(Wb[:, :, :], WH2).then_inc(S["wd"], 1)
            pool.wait_ge(S["wd"], 2)
            pool.tensor_tensor(Wb[F:P, :, :], WH2[F:P], Wa[F:P, :, :], ALU.subtract).then_inc(S["wd"], 1)
            pool.wait_ge(S["wd"], 3)

            def centre(ln):
                for i in range(NB):
                    n = NB * ln + i
                    pool.wait_ge(S["mean_sum"], n + 1)
                    pool.tensor_scalar(stat[:, i % 2, 1, :], stat[:, i % 2, 0, :], -1.0 / F, None, ALU.mult)\
                        .then_inc(S["mean_neg"], 1)
                    pool.wait_ge(S["mean_neg"], n + 1)
                    wait(pool, "x_ready", n - 1)
                    pool.tensor_tensor(groups(CEN[:, i % 2, :]), groups(R[:, i % 2, :]),
                                       stat[:, i % 2, 1, :].unsqueeze(2).broadcast_to([P, B, F]), ALU.add)\
                        .then_inc(S["cen"], 1)

            centre(0)

            pool.wait_ge(S["x_ready"], NB)

            def of_graph(at, u):
                return X[:, :, :].rearrange("p i (b f) -> p b i f", b=B)[:, at.graph(u)]

            def values_high(at, u):
                if u % H == 0:
                    pool.tensor_copy(XV[:, at.graph(u), :, 0:F], of_graph(at, u)).then_inc(S["xvh"], 1)

            def values_low(at, u):
                if u % H == 0:
                    b = at.graph(u)
                    pool.wait_ge(S["xvh"], b + 1)
                    pool.tensor_tensor(XV[:, b, :, F:P], of_graph(at, u), XV[:, b, :, 0:F], ALU.subtract)\
                        .then_inc(S["xvl"], 1)

            def negate(at, l):
                k = at.base + l
                wait_at_ends(pool, "s_exp", k - V_RING + 1)
                pool.wait_ge(S["s_max"], k + 1)
                r = l % V_RING
                pool.tensor_tensor(negm[:, r:r + 1], zero[:, :], mx[:, r:r + 1], ALU.subtract).then_inc(S["s_neg"], 1)

            def norm(at, l):
                wait(pool, "s_rec", at.base + l + 1)
                r = l % V_RING
                pool.tensor_scalar(PR[:, l % P_RING, :], PR[:, l % P_RING, :], rinv[:, r:r + 1], P_SCALE,
                                   ALU.mult, ALU.mult).then_inc(S["s_norm"], 1)

            def cat_low(at, u):
                pool.wait_ge(S["c_hi"], at.ubase + u + 1)
                pool.tensor_tensor(CL[:, u % 2, :], C32[:, u % 2, :], CH[:, u % 2, :], ALU.subtract).then_inc(S["c_lo"], 1)

            attention(pool, [(norm, "norm"), (negate, "negate")],
                      [(values_high, "values_high"), (values_low, "values_low"), (cat_low, "cat_low")], [])

            centre(1)
            for s, bias in ((2, bias2), (3, bias3)):
                pool.wait_ge(S["ld_b"], LD_B)
                pool.wait_ge(S["x_ready"], NB * s)
                for i in range(NB):
                    pool.tensor_tensor(groups(XB[:, i, :]), groups(X[:, i, :]),
                                       bias[:, :].unsqueeze(1).broadcast_to([P, B, F]), ALU.add).then_inc(S["xb"], 1)
                centre(s)

        @block.scalar
        def _(act):
            for j in range(NB):
                act.wait_ge(S["at_ps"], j + 1)
                act.activation(ATh[:, j, :], PS[:, j, :], ACT.Copy).then_inc(S["at_hi"], 1)
            for q in range(2):
                act.wait_ge(S["wt_ps"], q + 1)
                act.activation(WT[:, 4 * q:4 * q + 4, :], blocks(4 + q), ACT.Copy).then_inc(S["wt_sb"], 1)
            for q in range(2):
                act.wait_ge(S["g_ps"], q + 1)
                act.activation(GS[:, 4 * q:4 * q + 4, :], blocks(6 + q), ACT.Copy, scale=S_SCALE).then_inc(S["g_hi"], 1)

            def p_stage(s):
                def take_xt(p):
                    n = PAIRS * s + p
                    act.wait_ge(S["xt_ps"], n + 1)
                    wait(act, "proj_ps", n - 1)
                    act.activation(XT[:, n % 2, :], PS[:, 2 + n % 2, :], ACT.Copy).then_inc(S["xt_sb"], 1)
                take_xt(0)
                for p in range(PAIRS):
                    n = PAIRS * s + p
                    if p + 1 < PAIRS:
                        take_xt(p + 1)
                    act.wait_ge(S["proj_ps"], n + 1)
                    act.activation(Qh[:, QSET[A_OF_P[s]], :, cols(p)], blocks(4 + n % 2), ACT.Copy).then_inc(S["q_hi"], 1)

            def spread(ln, before):
                for i in range(NB + 1):
                    if i < NB:
                        before(i)
                    if i:
                        n = NB * ln + i - 1
                        e = (i - 1) % 2
                        act.wait_ge(S["cen"], n + 1)
                        wait(act, "var_sum", n)
                        act.activation(SQ, CEN[:, e, :], ACT.Square).then_inc(S["sq"], 1)
                        act.wait_ge(S["var_eps"], n + 1)
                        act.activation(stat[:, e, 4, :], stat[:, e, 3, :], ACT.Sqrt).then_inc(S["sd"], 1)

            p_stage(0)
            for i in range(NB):
                for c in (0, 1):
                    act.wait_ge(S["am_ps"], 2 * i + c + 1)
                    act.activation(Z[:, i, halfc(c)], PS[:, c, :], ACT.Relu, scale=1.0 / Q_SCALE).then_inc(S["am_ev"], 1)
            p_stage(1)

            def relu_out(i):
                wait(act, "r_ready", i - 1)
                for c in (0, 1):
                    act.wait_ge(S["am_ps"], 8 + 2 * i + c + 1)
                    act.activation(EV[:, i % 2, halfc(c)], PS[:, c, :], ACT.Relu, scale=1.0 / Q_SCALE).then_inc(S["am_ev"], 1)

            spread(0, relu_out)

            act.wait_ge(S["ld_b"], LD_B)
            act.activation(bhS[:, :], bhT[:, :], ACT.Copy, scale=SLOPE * P_SCALE).then_inc(S["bhs"], 1)
            act.activation(bhP[:, :], bhT[:, :], ACT.Copy, scale=P_SCALE).then_inc(S["bhs"], 1)
            act.wait_ge(S["bhs"], 2)
            act.wait_ge(S["x_ready"], NB)

            def twice(at, u):
                if u % H == 0:
                    b = at.graph(u)
                    wait(act, "pt_ps", b)
                    act.activation(XD, X[:, :, :].rearrange("p i (b f) -> p b i f", b=B)[:, b].unsqueeze(2)
                                   .broadcast_to([P, NB, 2, F]), ACT.Copy).then_inc(S["xd"], 1)

            def columns_high(at, u):
                if u % H == 0:
                    b = at.graph(u)
                    wait(act, "pt_ps", b + 1)
                    act.activation(XHH[:, b, :], bO, ACT.Copy).then_inc(S["xhh"], 1)

            def exps(at, l):
                k = at.base + l
                wait_at_ends(act, "t_ps", k - P_RING + 1)
                wait_at_ends(act, "s_rec", k - V_RING + 1)
                wait(act, "s_neg", k + 1)
                r = l % V_RING
                act.activation(PR[:, l % P_RING, :], TS[:, l % T_RING, :], ACT.Exp, bias=negm[:, r:r + 1],
                               accum_out=rsum[:, r:r + 1]).then_inc(S["s_exp"], 1)

            def probs_high(at, l):
                k = at.base + l
                u, i = l // NB, l % NB
                wait_at_ends(act, "av_ps", at.ubase + u - 1)
                wait(act, "t_ps", k + 1)
                act.activation(PH[:, u % 2, :, P * i:P * i + P], blocks(2 + l % 2), ACT.Copy).then_inc(S["p_hi"], 1)

            def left_high(at, u):
                g = at.ubase + u
                wait_at_ends(act, "s_ps", at.base + NB * (u - 1))
                wait(act, "y_ps", g + 1)
                act.activation(YS[:, u % 2, :], bY, ACT.Copy).then_inc(S["y_hi"], 1)

            def u_high(at, u):
                g = at.ubase + u
                wait_at_ends(act, "o_ps", g - 1)
                wait(act, "av_ps", g + 1)
                act.activation(UA[:, u % 2, :], bU, ACT.Copy).then_inc(S["u_hi"], 1)

            def cat_small(at, u):
                g = at.ubase + u
                h = u % H
                wait_at_ends(act, "c_sb", g)
                wait(act, "o_ps", g + 1)
                act.activation(CS, bO, ACT.Identity, bias=bhS[:, h:h + 1], scale=SLOPE).then_inc(S["c_small"], 1)

            def cat_high(at, u):
                g = at.ubase + u
                wait_at_ends(act, "h2_ps", g - 1)
                wait(act, "c_sb", g + 1)
                act.activation(CH[:, u % 2, :], C32[:, u % 2, :], ACT.Copy).then_inc(S["c_hi"], 1)

            def keep_high(at, u):
                if u % H == H - 1:
                    b = at.graph(u)
                    wait(act, "h2_ps", at.ubase + u + 1)
                    act.activation(H2h[:, b, :], bH, ACT.Copy, scale=H_SCALE / P_SCALE).then_inc(S["h2_hi"], 1)

            def h2_high(at, u):
                b = at.graph(u)
                wait(act, "s_ps", at.base + NB * (u - 1))
                wait(act, "pm_cols", b + 1)
                act.activation(YS[:, u % 2, :], bY, ACT.Copy).then_inc(S["y_hi"], 1)
                act.activation(XHH2[:, u % 2, :], bY, ACT.Copy).then_inc(S["xh2"], 1)

            def h2_rows_high(at, u):
                b = at.graph(u)
                wait(act, "av_ps", H * b + H)
                wait(act, "pm_rows", b + 1)
                act.activation(XV[:, b, :, 0:F], blocks(7)[:, :, 0:F], ACT.Copy).then_inc(S["xv2h"], 1)

            attention(act, [(probs_high, "probs_high"), (exps, "exps")],
                      [(twice, "twice"), (columns_high, "columns_high"), (left_high, "left_high"), (u_high, "u_high"),
                       (cat_small, "cat_small"), (cat_high, "cat_high"), (keep_high, "keep_high")],
                      [(h2_high, "h2_high"), (h2_rows_high, "h2_rows_high")])

            spread(1, lambda i: None)
            p_stage(2)
            for i in range(NB):
                act.wait_ge(S["am_ev"], 16 + 2 * i + 2)
                act.activation(Qh[:, 1, i, :], F1[:, i, :], ACT.Copy, scale=Q_SCALE).then_inc(S["q1_hi"], 1)
            spread(2, lambda i: None)
            p_stage(3)
            spread(3, lambda i: None)

        @block.vector
        def _(dve):
            dve.wait_ge(S["ld_adj"], 16)
            dve.tensor_scalar(MASK[:, :, :], ADJ, 0.0, NEG * S_SCALE, ALU.is_equal, ALU.mult).then_inc(S["adjx"], 1)
            dve.scalar_tensor_tensor(ADJX[:, :, :], ADJ, 0.0, ADJ, ALU.is_equal, ALU.add).then_inc(S["adjx"], 1)
            dve.wait_ge(S["adjx"], 2)
            dve.tensor_scalar(ADJX[:, :, :], ADJX[:, :, :], 1.0 / S_SCALE, None, ALU.mult).then_inc(S["adjx"], 1)
            dve.wait_ge(S["ld_w"], LD_W)
            dve.wait_ge(S["zeroed"], 3)
            dve.tensor_tensor(tmpw[:, 0, :], WRAW[:, 4, :], WRAW[:, 6, :], ALU.add).then_inc(S["bd_sum"], 1)
            dve.tensor_tensor(tmpw[:, 1, :], WRAW[:, 3, :], WRAW[:, 5, :], ALU.add).then_inc(S["bd_sum"], 1)
            dve.wait_ge(S["bd_sum"], 2)
            for half in (0, 1):
                r = slice(F * half, F * half + F)
                for k, src, scale in ((0, WRAW[r, 0, :], Q_SCALE), (1, WRAW[r, 1, :], Q_SCALE),
                                      (2, tmpw[r, 0, :], 2.0 * Q_SCALE), (3, tmpw[r, 1, :], 1.0),
                                      (5, WRAW[r, 7, :], 1.0), (6, WRAW[r, 8, :], Q_SCALE)):
                    dve.tensor_scalar(BD[r, k, r], src, scale, None, ALU.mult).then_inc(S["bd_ready"], 1)
                dve.tensor_tensor(BD[r, 4, r], WRAW[r, 2, :], tmpw[r, 0, :], ALU.subtract).then_inc(S["bd_ready"], 1)
            for j in range(NB):
                dve.wait_ge(S["at_hi"], j + 1)
                dve.tensor_tensor(ATl[:, j, :], PS[:, j, :], ATh[:, j, :], ALU.subtract).then_inc(S["at_lo"], 1)
            for q in range(2):
                dve.wait_ge(S["g_hi"], q + 1)
                dve.scalar_tensor_tensor(GS[F:P, 4 * q:4 * q + 4, :], blocks(6 + q)[F:P], S_SCALE,
                                         GS[F:P, 4 * q:4 * q + 4, :], ALU.mult, ALU.subtract).then_inc(S["g_lo"], 1)

            def p_stage(s):
                for p in range(PAIRS):
                    n = PAIRS * s + p
                    dve.wait_ge(S["proj_ps"], n + 1)
                    if s == 2:
                        dve.tensor_copy(F1[:, :, cols(p)], blocks(FB[0][n % 2])).then_inc(S["f_done"], 1)
                    if s >= 2:
                        dve.wait_ge(S["xb"], NB * (s - 1))
                        dve.tensor_tensor(XB[:, :, cols(p)], blocks(FB[len(PROJ[s]) - 2][n % 2]),
                                          XB[:, :, cols(p)], ALU.add).then_inc(S["f_done"], 1)
                    dve.wait_ge(S["q_hi"], n + 1)
                    a = QSET[A_OF_P[s]]
                    dve.tensor_tensor(Ql[:, a, :, cols(p)], blocks(4 + n % 2), Qh[:, a, :, cols(p)],
                                      ALU.subtract).then_inc(S["q_done"], 1)

            def norm_rows(ln, before):
                for i in range(NB + 1):
                    if i < NB:
                        n = NB * ln + i
                        e = i % 2
                        wait(dve, "cen", n - 1)
                        before(i)
                        dve.wait_ge(S["r_ready"], n + 1)
                        dve.reduce_sum(stat[:, e, 0, :], groups(R[:, e, :]), AX).then_inc(S["mean_sum"], 1)
                    if i:
                        n = NB * ln + i - 1
                        e = (i - 1) % 2
                        st = lambda k: stat[:, e, k, :]
                        dve.wait_ge(S["sq"], n + 1)
                        dve.reduce_sum(st(2), groups(SQ), AX).then_inc(S["var_sum"], 1)
                        dve.wait_ge(S["var_sum"], n + 1)
                        dve.tensor_scalar(st(3), st(2), 1.0 / F, EPS, ALU.mult, ALU.add).then_inc(S["var_eps"], 1)
                        dve.wait_ge(S["sd"], n + 1)
                        dve.reciprocal(st(5), st(4)).then_inc(S["rs"], 1)
                        dve.wait_ge(S["rs"], 4 * n + 1)
                        dve.tensor_tensor(st(6), st(5), st(5), ALU.mult).then_inc(S["rs"], 1)
                        dve.wait_ge(S["rs"], 4 * n + 2)
                        dve.scalar_tensor_tensor(st(6), st(6), -0.5, st(3), ALU.mult, ALU.mult).then_inc(S["rs"], 1)
                        dve.wait_ge(S["rs"], 4 * n + 3)
                        dve.scalar_tensor_tensor(st(7), st(6), 1.5, st(5), ALU.add, ALU.mult).then_inc(S["rs"], 1)
                        dve.wait_ge(S["rs"], 4 * n + 4)
                        dve.tensor_tensor(groups(X[:, i - 1, :]), groups(CEN[:, e, :]),
                                          st(7).unsqueeze(2).broadcast_to([P, B, F]), ALU.mult).then_inc(S["x_ready"], 1)

            p_stage(0)
            p_stage(1)

            def l0_sum(i):
                dve.wait_ge(S["am_ev"], 8 + 2 * i + 2)
                dve.tensor_tensor(R[:, i % 2, :], EV[:, i % 2, :], X[:, i, :], ALU.add).then_inc(S["r_ready"], 1)

            norm_rows(0, l0_sum)

            def columns_low(at, u):
                if u % H == 0:
                    b = at.graph(u)
                    wait(dve, "xhh", b + 1)
                    dve.tensor_tensor(XLL[:, b, :], bO, XHH[:, b, :], ALU.subtract).then_inc(S["xll"], 1)

            def scale_max(at, l):
                k = at.base + l
                wait_at_ends(dve, "s_exp", k - T_RING + 1)
                wait_at_ends(dve, "s_neg", k - V_RING + 1)
                wait_at_ends(dve, "s_ps", k + 1)
                r = l % V_RING
                dve.tensor_tensor_reduce(out=TS[:, l % T_RING, :], in0=bS[l % 2], in1=ADJX[:, l % NB, :],
                                         scale=1.0, scalar=-3.0e38, op0=ALU.mult, op1=ALU.max,
                                         accum_out=mx[:, r:r + 1]).then_inc(S["s_max"], 1)

            def recip(at, l):
                k = at.base + l
                wait_at_ends(dve, "s_norm", k - V_RING + 1)
                wait_at_ends(dve, "s_exp", k + 1)
                ahead = k + RECIP_AHEAD + 1
                wait(dve, "s_ps", min(ahead, TILES) if isinstance(ahead, int) else ahead)
                r = l % V_RING
                dve.reciprocal(rinv[:, r:r + 1], rsum[:, r:r + 1]).then_inc(S["s_rec"], 1)

            def probs_low(at, l):
                u, i = l // NB, l % NB
                wait(dve, "p_hi", at.base + l + 1)
                dve.tensor_tensor(PL[:, u % 2, :, P * i:P * i + P], blocks(2 + l % 2),
                                  PH[:, u % 2, :, P * i:P * i + P], ALU.subtract).then_inc(S["p_lo"], 1)

            def left_low(at, u):
                wait(dve, "y_hi", at.ubase + u + 1)
                dve.tensor_tensor(YS[F:P, u % 2, :], bY[F:P], YS[F:P, u % 2, :], ALU.subtract).then_inc(S["y_lo"], 1)

            def u_low(at, u):
                g = at.ubase + u
                wait_at_ends(dve, "o_ps", g - 1)
                wait(dve, "u_hi", g + 1)
                dve.tensor_tensor(UB[0:F, u % 2, :], bU[0:F], UA[0:F, u % 2, :], ALU.subtract).then_inc(S["u_lo"], 1)
                dve.tensor_copy(UB[F:P, u % 2, :], UA[0:F, u % 2, :]).then_inc(S["u_sb"], 1)

            def keep_low(at, u):
                if u % H == H - 1:
                    b = at.graph(u)
                    wait(dve, "h2_hi", b + 1)
                    dve.scalar_tensor_tensor(H2l[:, b, :], bH, H_SCALE / P_SCALE, H2h[:, b, :],
                                             ALU.mult, ALU.subtract).then_inc(S["h2_sb"], 1)

            def take_u(at, u):
                wait_at_ends(dve, "no_ps", at.graph(u) - 1)
                wait(dve, "av_ps", at.ubase + u + 1)
                dve.tensor_copy(US[:, u % 2, :], bU).then_inc(S["u_sb"], 1)

            def cat(at, u):
                g = at.ubase + u
                h = u % H
                wait_at_ends(dve, "c_lo", g - 1)
                wait(dve, "c_small", g + 1)
                dve.scalar_tensor_tensor(C32[:, u % 2, :], bO, bhP[:, h:h + 1], CS, ALU.add, ALU.max).then_inc(S["c_sb"], 1)

            def h2_low(at, u):
                b = at.graph(u)
                wait(dve, "xh2", b + 1)
                left_low(at, u)
                dve.tensor_tensor(XLL2[:, u % 2, :], bY, XHH2[:, u % 2, :], ALU.subtract).then_inc(S["xl2"], 1)

            def h2_rows_low(at, u):
                b = at.graph(u)
                wait(dve, "xv2h", b + 1)
                dve.tensor_tensor(XV[:, b, :, F:P], blocks(7)[:, :, F:P], XV[:, b, :, 0:F],
                                  ALU.subtract).then_inc(S["xv2l"], 1)

            def take_out(at, u):
                b = at.graph(u)
                wait(dve, "no_ps", b + 1)
                dve.tensor_tensor(G2.rearrange("p i (b f) -> p b i f", b=B)[:, b],
                                  bO[:, 0:NB * F].rearrange("p (i f) -> p i f", i=NB),
                                  bout[:, :].unsqueeze(1).broadcast_to([P, NB, F]), ALU.add).then_inc(S["g2"], 1)

            attention(dve, [(scale_max, "scale_max"), (recip, "recip"), (probs_low, "probs_low")],
                      [(columns_low, "columns_low"), (left_low, "left_low"), (u_low, "u_low"), (cat, "cat"),
                       (keep_low, "keep_low")],
                      [(h2_low, "h2_low"), (h2_rows_low, "h2_rows_low"), (take_u, "take_u"),
                       (take_out, "take_out")])

            def l1_sum(i):
                dve.scalar_tensor_tensor(EV[:, i % 2, :], G2[:, i, :], SLOPE, G2[:, i, :], ALU.mult, ALU.max)\
                    .then_inc(S["lr"], 1)
                dve.wait_ge(S["lr"], i + 1)
                dve.tensor_tensor(R[:, i % 2, :], EV[:, i % 2, :], X[:, i, :], ALU.add).then_inc(S["r_ready"], 1)

            dve.wait_ge(S["ld_b"], LD_B)
            dve.wait_ge(S["g2"], B)
            norm_rows(1, l1_sum)
            p_stage(2)
            for i in range(NB):
                for c in (0, 1):
                    dve.wait_ge(S["am_ps"], 16 + 2 * i + c + 1)
                    dve.scalar_tensor_tensor(F1[:, i, halfc(c)], PS[:, c, :], 1.0 / Q_SCALE, F1[:, i, halfc(c)],
                                             ALU.mult, ALU.add).then_inc(S["am_ev"], 1)
                if i:
                    dve.wait_ge(S["q1_hi"], i)
                    dve.scalar_tensor_tensor(Ql[:, 1, i - 1, :], F1[:, i - 1, :], Q_SCALE, Qh[:, 1, i - 1, :],
                                             ALU.mult, ALU.subtract).then_inc(S["q1_lo"], 1)
            dve.wait_ge(S["q1_hi"], NB)
            dve.scalar_tensor_tensor(Ql[:, 1, NB - 1, :], F1[:, NB - 1, :], Q_SCALE, Qh[:, 1, NB - 1, :],
                                     ALU.mult, ALU.subtract).then_inc(S["q1_lo"], 1)

            def sum_of(a):
                def sum_rows(i):
                    for c in (0, 1):
                        dve.wait_ge(S["am_ps"], 8 * a + 2 * i + c + 1)
                        ins = dve.scalar_tensor_tensor(R[:, i % 2, halfc(c)], PS[:, c, :], 1.0 / Q_SCALE,
                                                       XB[:, i, halfc(c)], ALU.mult, ALU.add)
                        ins.then_inc(S["am_ev"], 1)
                    dve.wait_ge(S["am_ev"], 8 * a + 2 * i + 2)
                    dve.engine_nop().then_inc(S["r_ready"], 1)
                return sum_rows

            norm_rows(2, sum_of(3))
            p_stage(3)
            norm_rows(3, sum_of(4))

        @block.tensor
        def _(pe):
            pe.wait_ge(S["ld_adj"], 16)
            pe.wait_ge(S["consts"], 8)
            for j in range(NB):
                for i in range(NB):
                    last = pe.transpose(PS[:, j, P * i:P * i + P], ADJ[:, i, P * j:P * j + P], ident[:, :])
                last.then_inc(S["at_ps"], 1)
            pe.wait_ge(S["ld_w"], LD_W)
            for q in range(2):
                for k in range(4):
                    last = pe.transpose(blocks(4 + q)[:, k, :], WH2[:, 4 * q + k, :], ident[:, :])
                last.then_inc(S["wt_ps"], 1)
            for q in range(2):
                pe.wait_ge(S["wt_sb"], q + 1)
                for k in range(4):
                    last = pe.matmul(blocks(6 + q)[:, k, :], WT[:, 4 * q + k, :], WT[:, 4 * q + k, :],
                                     start=True, stop=True)
                last.then_inc(S["g_ps"], 1)
            pe.wait_ge(S["at_lo"], NB)
            pe.wait_ge(S["wt_sb"], 2)
            pe.wait_ge(S["bd_ready"], 14)

            def p_stage(s):
                src = Z if s == 1 else X

                def turn(p):
                    n = PAIRS * s + p
                    wait(pe, "xt_sb", n - 1)
                    for i in range(NB):
                        last = pe.transpose(blocks(2 + n % 2)[:, i, :], src[:, i, cols(p)], ident[:, :])
                    last.then_inc(S["xt_ps"], 1)

                turn(0)
                for p in range(PAIRS):
                    n = PAIRS * s + p
                    if p + 1 < PAIRS:
                        turn(p + 1)
                    pe.wait_ge(S["xt_sb"], n + 1)
                    wait(pe, "q_done", n - 1)
                    for k, w in enumerate(PROJ[s]):
                        bank = 4 + n % 2 if k == 0 else FB[k - 1][n % 2]
                        for i in range(NB):
                            last = pe.matmul(blocks(bank)[:, i, :], XT[:, n % 2, P * i:P * i + P], BD[:, w, :],
                                             start=True, stop=True)
                    last.then_inc(S["proj_ps"], 1)

            def a_stage(a):
                q = QSET[a]

                def rows(i, m, first):
                    for c in (0, 1):
                        if not first:
                            pe.wait_ge(S["am_ev"], m + c - 1)
                        for k in range(3 * NB):
                            j, way = k % NB, k // NB
                            left = ATl if way == 2 else ATh
                            right = Ql if way == 1 else Qh
                            last = pe.matmul(PS[:, c, :], left[:, j, bass.ds(P * i, P)], right[:, q, j, halfc(c)],
                                             start=(k == 0), stop=(k == 3 * NB - 1))
                        last.then_inc(S["am_ps"], 1)

                rows(0, 8 * a, a == 0)
                with pe.Fori(1, NB) as i:
                    rows(i, 8 * a + 2 * i, False)

            pe.wait_ge(S["ld_x"], 16 * NB)
            p_stage(0)
            pe.wait_ge(S["q_done"], PAIRS)
            a_stage(0)
            pe.wait_ge(S["am_ev"], 8)
            p_stage(1)
            pe.wait_ge(S["q_done"], 2 * PAIRS)
            a_stage(1)

            pe.wait_ge(S["g_lo"], 2)
            pe.wait_ge(S["wo"], 2)
            pe.wait_ge(S["wd"], 3)
            pe.wait_ge(S["adjx"], 3)

            def columns(at, u):
                if u % H == 0:
                    b = at.graph(u)
                    wait(pe, "c_sb", at.ubase + u - 5)
                    wait(pe, "xd", b + 1)
                    for i in range(NB):
                        last = pe.transpose(blocks(5)[:, i, :], XD[:, i].rearrange("p t f -> p (t f)"), ident[:, :])
                    last.then_inc(S["pt_ps"], 1)

            def scores(at, l):
                k = at.base + l
                u, i = l // NB, l % NB
                if at.heads:
                    if i == 0:
                        wait(pe, "y_lo", at.ubase + u + 1)
                    hi, lo = XHH[:, at.graph(u), :], XLL[:, at.graph(u), :]
                else:
                    if i == 0:
                        wait(pe, "y_lo", at.ubase + u + 1)
                        wait(pe, "xl2", at.graph(u) + 1)
                    hi, lo = XHH2[:, u % 2, :], XLL2[:, u % 2, :]
                wait(pe, "s_max", k - 1)
                pe.matmul(bS[l % 2], identb[:, :], MASK[:, i, :], start=True, stop=False)
                pe.matmul(bS[l % 2], YS[:, u % 2, P * i:P * i + P], hi, start=False, stop=False)
                pe.matmul(bS[l % 2], YS[:, u % 2, P * i:P * i + P], lo, start=False, stop=True)\
                    .then_inc(S["s_ps"], 1)

            def turn_probs(at, l):
                k = at.base + l
                wait_at_ends(pe, "p_lo", k - 1)
                wait(pe, "s_norm", k + 1)
                for j in range(NB):
                    last = pe.transpose(blocks(2 + l % 2)[:, j, :], PR[:, l % P_RING, P * j:P * j + P], ident[:, :])
                last.then_inc(S["t_ps"], 1)

            def left_proj(at, u):
                g = at.ubase + u
                wait(pe, "y_lo", g)
                if u % H == 0:
                    wait(pe, "xll", at.graph(u) + 1)
                pe.matmul(bY, GS[:, u % H, :], XHH[:, at.graph(u), :], start=True, stop=False)
                pe.matmul(bY, GS[:, u % H, :], XLL[:, at.graph(u), :], start=False, stop=True).then_inc(S["y_ps"], 1)

            def times_values(at, u):
                g = at.ubase + u
                wait_at_ends(pe, "u_sb", g)
                if not at.heads:
                    wait(pe, "xv2l", at.graph(u) + 1)
                elif u % H == 0:
                    wait(pe, "xvl", at.graph(u) + 1)
                wait(pe, "p_lo", at.base + NB * u + NB)
                for j in range(NB):
                    v = XV[:, at.graph(u), j, :]
                    pe.matmul(bU, v, PH[:, u % 2, j, :], start=(j == 0), stop=False)
                    last = pe.matmul(bU, v, PL[:, u % 2, j, :], start=False, stop=(j == NB - 1))
                last.then_inc(S["av_ps"], 1)

            def head_out(at, u):
                g = at.ubase + u
                wait_at_ends(pe, "c_sb", g)
                if u == -5 and at.it is not B:
                    wait(pe, "xll", at.graph(u) + 2)
                wait(pe, "u_sb", g + 1)
                pe.matmul(bO, Wa[:, u % H, :], UA[:, u % 2, :], start=True, stop=False)
                pe.matmul(bO, Wb[:, u % H, :], UB[:, u % 2, :], start=False, stop=True).then_inc(S["o_ps"], 1)

            def add_h2(at, u):
                h = u % H
                if h == 0:
                    wait(pe, "h2_sb", at.graph(u))
                wait(pe, "c_lo", at.ubase + u + 1)
                pe.matmul(bH, WO[:, h, :], CH[:, u % 2, :], start=(h == 0), stop=False)
                pe.matmul(bH, WO[:, h, :], CL[:, u % 2, :], start=False, stop=(h == H - 1)).then_inc(S["h2_ps"], 1)

            def sum_h2(at, u):
                b = at.graph(u)
                wait(pe, "h2_sb", b + 1)
                wait(pe, "y_lo", H * B)
                wait(pe, "xv2l", b)
                pe.matmul(bY, IIh[:, :], H2h[:, b, :], start=True, stop=False)
                pe.matmul(bY, IIh[:, :], H2l[:, b, :], start=False, stop=True).then_inc(S["pm_cols"], 1)

            def sum_h2_rows(at, u):
                b = at.graph(u)
                wait(pe, "xl2", b + 1)
                for i in range(NB):
                    pe.matmul(blocks(7)[:, i, :], H2h[:, b, P * i:P * i + P], IIh[:, :], start=True, stop=False)
                    last = pe.matmul(blocks(7)[:, i, :], H2l[:, b, P * i:P * i + P], IIh[:, :],
                                     start=False, stop=True)
                last.then_inc(S["pm_rows"], 1)

            def rows_out(at, u):
                b = at.graph(u)
                wait(pe, "c_sb", H * B)
                wait(pe, "g2", b)
                wait(pe, "u_sb", at.ubase + u + 1)
                for i in range(NB):
                    last = pe.matmul(bO[:, F * i:F * i + F], US[:, u % 2, P * i:P * i + P], IIs[:, :],
                                     start=True, stop=True)
                last.then_inc(S["no_ps"], 1)

            attention(pe, [(scores, "scores"), (turn_probs, "turn_probs")],
                      [(columns, "columns"), (left_proj, "left_proj"), (times_values, "times_values"),
                       (head_out, "head_out"), (add_h2, "add_h2")],
                      [(sum_h2, "sum_h2"), (sum_h2_rows, "sum_h2_rows"), (times_values, "times_values"),
                       (rows_out, "rows_out")])

            pe.wait_ge(S["x_ready"], 2 * NB)
            p_stage(2)
            pe.wait_ge(S["q_done"], 3 * PAIRS)
            a_stage(2)
            pe.wait_ge(S["q1_lo"], NB)
            a_stage(3)
            pe.wait_ge(S["x_ready"], 3 * NB)
            p_stage(3)
            pe.wait_ge(S["q_done"], 4 * PAIRS)
            a_stage(4)


_INS = ["x", "adj", "L0_gnn_net_params", "L1_gnn_Wh", "L1_gnn_bh", "L1_gnn_W_out", "L1_gnn_b_out",
        "L2_gnn_weight", "L2_gnn_bias", "L3_gnn_weight_self", "L3_gnn_weight_neighbor", "L3_gnn_bias"]


def kernel(**inputs):
    import numpy as _np
    import concourse.bacc as _bacc
    from concourse import mybir as _mybir
    from concourse.bass_utils import run_bass_kernel_spmd as _run

    nc = _bacc.Bacc("TRN2", target_bir_lowering=False, num_devices=1)
    arrays, args = {}, []
    for name in _INS:
        a = _np.ascontiguousarray(inputs[name])
        arrays[f"in_{name}_dram"] = a
        args.append(nc.dram_tensor(f"in_{name}_dram", a.shape, _mybir.dt.from_np(a.dtype), kind="ExternalInput").ap())
    args.append(nc.dram_tensor("out_0_dram", (B, N, F), _mybir.dt.float32, kind="ExternalOutput").ap())
    build(nc, *args)
    r = _run(nc, [arrays], core_ids=[0])
    return r.results[0]["out_0_dram"]
```

```python
from contextlib import ExitStack

import concourse.bass as bass
from concourse import mybir

ALU = mybir.AluOpType
ACT = mybir.ActivationFunctionType
F32 = mybir.dt.float32
F16 = mybir.dt.float16
BF16 = mybir.dt.bfloat16
AX = mybir.AxisListType.X

P = 128
B = 16
N = 512
F = 64
NB = N // P
H = 8
D = 128
PAIRS = B // 2
COLS = B * F
EPS = 1e-5
SLOPE = 0.01
NEG = -1e16
S_SCALE = 2.0 ** -6
P_SCALE = 2.0 ** 4
H_SCALE = 2.0 ** -3
Q_SCALE = 2.0 ** -4

ARENA = 39936
SEMAPHORES = """
    ld_adj ld_x ld_x2 ld_w ld_b stored
    zeroed consts bd_sum bd_ready wo wd adjx
    at_ps at_hi at_lo wt_ps wt_sb g_ps g_hi g_lo
    xt_ps xt_sb proj_ps q_hi q_done f_done am_ps am_ev xb q1_hi q1_lo
    r_ready mean_sum mean_neg cen sq var_sum var_eps sd rs newton x_rows
    half_neg half_cen half_newton x_halves
    us_sb xd xvh xvl pt_ps u_hi u_lo h2_hi xhh xll
    y_ps y_hi y_lo s_ps s_max s_neg s_exp s_rec s_norm t_ps p_hi p_lo
    av_ps u_sb o_ps bhs c_small c_sb c_hi c_lo h2_ps h2_sb
    pm_cols pm_rows xh2 xl2 xv2h xv2l no_ps g2 lr r1
"""

LAG = {
    "scores": 11.2, "turn_probs": 17.7,
    "left_proj": 9.4, "times_values": 23.3, "head_out": 25.6, "add_h2": 31.8,
    "columns": 4.1,
    "exps": 15.0, "probs_high": 17.9,
    "left_high": 9.2, "u_high": 23.4, "cat_small": 25.4, "cat_high": 26.9,
    "twice": 2.7, "columns_high": 4.4, "keep_high": 32.1,
    "scale_max": 12.0, "recip": 16.95, "probs_low": 18.9,
    "left_low": 10.3, "u_low": 24.3, "cat": 26.8,
    "columns_low": 5.4, "keep_low": 35.3,
    "negate": 11.3, "norm": 15.9,
    "cat_low": 27.4, "values_high": 5.8, "values_low": 5.9,
    "sum_h2": 9.2, "sum_h2_rows": 10.7, "out_values": 23.5, "rows_out": 25.4,
    "h2_high": 9.1, "h2_left_high": 9.4, "h2_rows_high": 10.4, "take_u": 23.5,
    "h2_low": 10.0, "h2_left_low": 10.1, "h2_rows_low": 12.3, "take_out": 27.2,
    "leaky": 28.3, "add_x": 29.4,
}
TAIL = 40
T_RING = 8
P_RING = 8
V_RING = 8
HEAD_SLOTS = NB * H
HB = B // 2
PIECES = [(i, i + 1, 0, B) for i in range(NB - 1)] + [(NB - 1, NB, 0, HB), (NB - 1, NB, HB, B)]
PIECES_1 = [(0, 2, 0, HB), (2, NB, 0, HB), (0, 2, HB, B), (2, 3, HB, B), (3, NB, HB, B)]
LN_PIECES = len(PIECES)
WHOLE = NB - 1
HALVES = LN_PIECES - WHOLE
TILES = NB * B * (H + 1)
RECIP_AHEAD = 5


def build(nc, x, adj, net, wh, bh, w_out, b_out, w2, b2, w_self, w_nb, b3, out):
    with ExitStack() as ctx:
        def sb(name, shape, dt):
            return ctx.enter_context(nc.sbuf_tensor(name, shape, dt))

        X = sb("X", [P, NB, COLS], F32)
        ADJX = sb("ADJX", [P, NB, N], F32)
        MASK = sb("MASK", [P, NB, N], BF16)
        ATh = sb("ATh", [P, NB, N], F16)
        ATl = sb("ATl", [P, NB, N], F16)
        BD = sb("BD", [P, 7, P], F32)
        ident = sb("ident", [P, P], F32)
        identb = sb("identb", [P, P], BF16)
        IIh = sb("IIh", [P, P], F16)
        II = sb("II", [P, P], F32)
        IIs = sb("IIs", [P, F], F32)
        bout = sb("bout", [P, F], F32)
        bias2 = sb("bias2", [P, F], F32)
        bias3 = sb("bias3", [P, F], F32)
        bhT = sb("bhT", [P, H], F32)
        bhP = sb("bhP", [P, H], F32)
        bhS = sb("bhS", [P, H], F32)
        GS = sb("GS", [P, H, P], F16)
        Wa = sb("Wa", [P, H, D], F16)
        Wb = sb("Wb", [P, H, D], F16)
        WO = sb("WO", [P, H, P], F16)
        zero = sb("zero", [P, 1], F32)
        mx = sb("mx", [P, V_RING], F32)
        negm = sb("negm", [P, V_RING], F32)
        rsum = sb("rsum", [P, V_RING], F32)
        rinv = sb("rinv", [P, V_RING], F32)

        arena = sb("arena", [P, ARENA], F32)
        top = [0]

        def part(words, dt=F32):
            a = arena[:, top[0]:top[0] + words]
            top[0] += words
            assert top[0] <= ARENA, top[0]
            return a if dt == F32 else a.bitcast(dt)

        ADJ = part(NB * N).rearrange("p (i m) -> p i m", i=NB)
        WRAW = part(9 * F).rearrange("p (k f) -> p k f", k=9)
        WH2 = part(H * D).rearrange("p (h d) -> p h d", h=H)
        WT = part(H * P).rearrange("p (h d) -> p h d", h=H)
        WOR = part(H * F).rearrange("p (h d) -> p h d", h=H)
        tmpw = part(2 * F).rearrange("p (k f) -> p k f", k=2)
        Qh = part(NB * COLS, F16).rearrange("p (s j c) -> p s j c", s=2, j=NB)
        Ql = part(NB * COLS, F16).rearrange("p (s j c) -> p s j c", s=2, j=NB)
        XT = part(2 * N).rearrange("p (e n) -> p e n", e=2)
        Z = part(NB * COLS).rearrange("p (i c) -> p i c", i=NB)
        F1 = Z
        XB = part(NB * COLS).rearrange("p (i c) -> p i c", i=NB)
        EV = part(2 * COLS).rearrange("p (e c) -> p e c", e=2)
        R = part(NB * COLS).rearrange("p (i c) -> p i c", i=NB)
        CEN = part(NB * COLS).rearrange("p (i c) -> p i c", i=NB)
        SQ = part(NB * COLS).rearrange("p (i c) -> p i c", i=NB)
        stat = part(NB * 8 * B).rearrange("p (i k b) -> p i k b", i=NB, k=8)
        top[0] = 0
        XHH = part(B * N // 2, F16).rearrange("p (b n) -> p b n", b=B)
        G2 = arena[:, 0:NB * COLS].rearrange("p (i c) -> p i c", i=NB)
        XLL = part(B * N // 2, F16).rearrange("p (b n) -> p b n", b=B)
        XV = part(B * N // 2, F16).rearrange("p (b j c) -> p b j c", b=B, j=NB)
        PH = part(N * NB, F16).rearrange("p (e j n) -> p e j n", e=2, j=NB)
        PL = part(N * NB, F16).rearrange("p (e j n) -> p e j n", e=2, j=NB)
        H2h = part(B * N // 2, F16).rearrange("p (b n) -> p b n", b=B)
        H2l = part(B * N // 2, F16).rearrange("p (b n) -> p b n", b=B)
        PR = part(P_RING * N).rearrange("p (r m) -> p r m", r=P_RING)
        TS = part(T_RING * N).rearrange("p (r m) -> p r m", r=T_RING)
        US = part(2 * N).rearrange("p (e n) -> p e n", e=2)
        UA = part(N, F16).rearrange("p (e n) -> p e n", e=2)
        UB = part(N, F16).rearrange("p (e n) -> p e n", e=2)
        CS = part(N)
        C32 = part(2 * N).rearrange("p (e n) -> p e n", e=2)
        CH = part(N, F16).rearrange("p (e n) -> p e n", e=2)
        CL = part(N, F16).rearrange("p (e n) -> p e n", e=2)
        YS = part(N, F16).rearrange("p (e n) -> p e n", e=2)
        XD = part(N).rearrange("p (i t f) -> p i t f", i=NB, t=2)
        LR = XD[:, :, 0, :]
        XHH2 = part(N, F16).rearrange("p (e n) -> p e n", e=2)
        XLL2 = part(N, F16).rearrange("p (e n) -> p e n", e=2)

        PS = ctx.enter_context(nc.psum_tensor("PS", [P, 8, N], F32))
        bS = [PS[:, 0, :], PS[:, 1, :]]
        bT = [PS[:, 2, :], PS[:, 3, :]]
        bU, bO, bH, bY = PS[:, 4, :], PS[:, 5, :], PS[:, 6, :], PS[:, 7, :]

        S = {name: ctx.enter_context(nc.semaphore(name)) for name in SEMAPHORES.split()}

        def wait(eng, name, value):
            if isinstance(value, int) and value <= 0:
                return
            eng.wait_ge(S[name], value)
            if eng is nc.gpsimd and not isinstance(value, int):
                eng.nop(nofuse=True)

        def wait_at_ends(eng, name, value):
            if isinstance(value, int):
                wait(eng, name, value)

        block = ctx.enter_context(nc.Block())

        class At:
            def __init__(self, phase, it):
                self.heads = phase == "heads"
                self.it = it
                self.base = HEAD_SLOTS * it if self.heads else 2 * NB * it + HEAD_SLOTS * B
                self.ubase = H * it if self.heads else 2 * it + H * B

            def graph(self, u):
                return self.it + u // H if self.heads else 2 * self.it + u

        def slot(s, bodies):
            turns = []
            for n, (at, tile_ops, unit_ops, low, high) in enumerate(bodies):
                for ops, every in ((tile_ops, 1), (unit_ops, NB)):
                    for op, name in ops:
                        first = s - int(LAG[name])
                        if first % every == 0 and low <= first < high:
                            turns.append((LAG[name] % 1, n, len(turns), op, at, first // every))
            for *_, op, at, index in sorted(turns, key=lambda t: t[:3]):
                op(at, index)

        def attention(eng, tile_ops, head_ops, out_ops):
            far = 1 << 20
            for s in range(HEAD_SLOTS):
                slot(s, [(At("heads", 0), tile_ops, head_ops, 0, far)])
            with eng.Fori(1, B) as it:
                for s in range(HEAD_SLOTS):
                    slot(s, [(At("heads", it), tile_ops, head_ops, -far, far)])
            for s in range(TAIL):
                slot(s, [(At("heads", B), tile_ops, head_ops, -far, 0),
                         (At("out", 0), tile_ops, out_ops, 0, far)])
            with eng.Fori(TAIL // (2 * NB), B // 2) as it:
                for s in range(2 * NB):
                    slot(s, [(At("out", it), tile_ops, out_ops, -far, far)])
            for s in range(TAIL):
                slot(s, [(At("out", B // 2), tile_ops, out_ops, -far, 0)])

        def groups(ap):
            return ap.rearrange("p (b f) -> p b f", b=B)

        def normed(eng, ln, k):
            if k < WHOLE:
                eng.wait_ge(S["x_rows"], WHOLE * ln + k + 1)
            else:
                eng.wait_ge(S["x_halves"], HALVES * ln + k - WHOLE + 1)

        @block.sync
        def _(sp):
            sp.dma_start(ADJ, adj.rearrange("(i p) m -> p i m", p=P)).then_inc(S["ld_adj"], 16)
            for half in (0, 1):
                rows = slice(F * half, F * half + F)
                sp.dma_start(WRAW[rows, 0:2, :], net.rearrange("(l f g) -> f l g", f=F, g=F)).then_inc(S["ld_w"], 16)
                sp.dma_start(WRAW[rows, 2:7, :], w2.rearrange("(k f) o -> f k o", f=F)).then_inc(S["ld_w"], 16)
                sp.dma_start(WRAW[rows, 7, :], w_self).then_inc(S["ld_w"], 16)
                sp.dma_start(WRAW[rows, 8, :], w_nb).then_inc(S["ld_w"], 16)
                sp.dma_start(WH2[rows, :, :], wh.rearrange("h c d -> c h d")).then_inc(S["ld_w"], 16)
            sp.dma_start(WOR, w_out.rearrange("(h d) o -> d h o", d=D)).then_inc(S["ld_w"], 16)
            for low, loaded in ((0, "ld_x"), (B // 2, "ld_x2")):
                graphs = slice(low, low + B // 2)
                for i in range(NB):
                    sp.dma_start(groups(X[:, i, :])[:, graphs],
                                 x.rearrange("b (i p) f -> i p b f", p=P)[i, :, graphs]).then_inc(S[loaded], 16)
            sp.dma_start(bhT[:, :], bh.rearrange("h d -> d h"), allow_slow_non_contiguous=True).then_inc(S["ld_b"], 16)
            for dst, src in ((bout, b_out), (bias2, b2), (bias3, b3)):
                sp.dma_start(dst[:, :], src.rearrange("(a f) -> a f", a=1).broadcast_to([P, F])).then_inc(S["ld_b"], 16)
            for k, (i, _end, low, high) in enumerate(PIECES):
                normed(sp, 3, k)
                sp.dma_start(out.rearrange("b (i p) f -> i p b f", p=P)[i, :, low:high],
                             groups(X[:, i, :])[:, low:high]).then_inc(S["stored"], 16)
            sp.wait_ge(S["stored"], 16 * LN_PIECES)

        LD_W = 11 * 16
        LD_B = 4 * 16
        PROJ = [[0], [1], [2, 3, 4], [6, 5]]
        FB = [[6, 7], [0, 1]]
        A_OF_P = [0, 1, 2, 4]
        QSET = [0, 1, 0, 1, 0]
        HALF = COLS // 2

        def cols(p):
            return slice(P * p, P * p + P)

        def halfc(c):
            return slice(HALF * c, HALF * c + HALF)

        def blocks(bank):
            return PS[:, bank, :].rearrange("p (i c) -> p i c", i=NB)

        def piece(buffer, ln, k):
            first, end, low, high = (PIECES_1 if ln == 1 else PIECES)[k]
            return buffer[:, first:end, low * F:high * F].rearrange("p i (b f) -> p i b f", f=F)

        def summed(ln, k):
            return piece(G2 if ln == 1 else R, ln, k)

        def st(ln, k, row):
            first, end, low, high = (PIECES_1 if ln == 1 else PIECES)[k]
            return stat[:, first:end, row, low:high]

        def over_features(ap):
            return ap.unsqueeze(3).broadcast_to([P, ap.shape[1], ap.shape[2], F])

        @block.gpsimd
        def _(pool):
            pool.memset(ident[:, :], 0.0).then_inc(S["zeroed"], 1)
            pool.memset(II[:, :], 0.0).then_inc(S["zeroed"], 1)
            pool.memset(zero[:, :], 0.0).then_inc(S["consts"], 1)
            pool.memset(BD[:, :, :], 0.0).then_inc(S["zeroed"], 1)
            pool.wait_ge(S["zeroed"], 3)
            pool.affine_select(out=ident[:, :], in_=ident[:, :], compare_op=ALU.not_equal, fill=1.0,
                               base=0, pattern=[[-1, P]], channel_multiplier=1).then_inc(S["consts"], 1)
            for k, base in enumerate((0, F, -F)):
                pool.wait_ge(S["consts"], 2 + k)
                pool.affine_select(out=II[:, :], in_=II[:, :], compare_op=ALU.not_equal, fill=1.0,
                                   base=base, pattern=[[-1, P]], channel_multiplier=1).then_inc(S["consts"], 1)
            pool.wait_ge(S["consts"], 5)
            pool.tensor_copy(identb[:, :], ident[:, :]).then_inc(S["consts"], 1)
            pool.tensor_copy(IIh[:, :], II[:, :]).then_inc(S["consts"], 1)
            pool.tensor_scalar(IIs[:, :], II[:, 0:F], 1.0 / (P_SCALE * H_SCALE), None, ALU.mult).then_inc(S["consts"], 1)
            pool.wait_ge(S["ld_w"], LD_W)
            pool.tensor_copy(WO[:, :, 0:F], WOR).then_inc(S["wo"], 1)
            pool.wait_ge(S["wo"], 1)
            pool.tensor_tensor(WO[:, :, F:P], WOR, WO[:, :, 0:F], ALU.subtract).then_inc(S["wo"], 1)
            pool.tensor_copy(Wa[:, :, :], WH2).then_inc(S["wd"], 1)
            pool.tensor_copy(Wb[:, :, :], WH2).then_inc(S["wd"], 1)
            pool.wait_ge(S["wd"], 2)
            pool.tensor_tensor(Wb[F:P, :, :], WH2[F:P], Wa[F:P, :, :], ALU.subtract).then_inc(S["wd"], 1)
            pool.wait_ge(S["wd"], 3)

            def whole_rows(ln):
                for k in range(WHOLE + 1):
                    if k < WHOLE:
                        n = WHOLE * ln + k
                        pool.wait_ge(S["mean_sum"], LN_PIECES * ln + k + 1)
                        pool.tensor_scalar(st(ln, k, 1), st(ln, k, 0), -1.0 / F, None, ALU.mult).then_inc(S["mean_neg"], 1)
                        pool.wait_ge(S["mean_neg"], n + 1)
                        pool.tensor_tensor(piece(CEN, ln, k), summed(ln, k), over_features(st(ln, k, 1)), ALU.add)\
                            .then_inc(S["cen"], 1)
                    if k:
                        q = k - 1
                        n = WHOLE * ln + q
                        pool.wait_ge(S["rs"], n + 1)
                        pool.tensor_tensor(st(ln, q, 6), st(ln, q, 5), st(ln, q, 5), ALU.mult).then_inc(S["newton"], 1)
                        pool.wait_ge(S["newton"], 4 * n + 1)
                        pool.tensor_tensor(st(ln, q, 6), st(ln, q, 6), st(ln, q, 3), ALU.mult).then_inc(S["newton"], 1)
                        pool.wait_ge(S["newton"], 4 * n + 2)
                        pool.tensor_scalar(st(ln, q, 6), st(ln, q, 6), -0.5, 1.5, ALU.mult, ALU.add).then_inc(S["newton"], 1)
                        pool.wait_ge(S["newton"], 4 * n + 3)
                        pool.tensor_tensor(st(ln, q, 7), st(ln, q, 6), st(ln, q, 5), ALU.mult).then_inc(S["newton"], 1)
                        pool.wait_ge(S["newton"], 4 * n + 4)
                        pool.tensor_tensor(piece(X, ln, q), piece(CEN, ln, q), over_features(st(ln, q, 7)),
                                           ALU.mult).then_inc(S["x_rows"], 1)

            whole_rows(0)

            pool.wait_ge(S["x_rows"], WHOLE)
            pool.wait_ge(S["x_halves"], HALVES)

            def of_graph(at, u):
                return X[:, :, :].rearrange("p i (b f) -> p b i f", b=B)[:, at.graph(u)]

            def values_high(at, u):
                if u % H == 0:
                    pool.tensor_copy(XV[:, at.graph(u), :, 0:F], of_graph(at, u)).then_inc(S["xvh"], 1)

            def values_low(at, u):
                if u % H == 0:
                    b = at.graph(u)
                    pool.wait_ge(S["xvh"], b + 1)
                    pool.tensor_tensor(XV[:, b, :, F:P], of_graph(at, u), XV[:, b, :, 0:F], ALU.subtract)\
                        .then_inc(S["xvl"], 1)

            def negate(at, l):
                k = at.base + l
                wait_at_ends(pool, "s_exp", k - V_RING + 1)
                pool.wait_ge(S["s_max"], k + 1)
                r = l % V_RING
                pool.tensor_tensor(negm[:, r:r + 1], zero[:, :], mx[:, r:r + 1], ALU.subtract).then_inc(S["s_neg"], 1)

            def norm(at, l):
                wait(pool, "s_rec", at.base + l + 1)
                r = l % V_RING
                pool.tensor_scalar(PR[:, l % P_RING, :], PR[:, l % P_RING, :], rinv[:, r:r + 1], P_SCALE,
                                   ALU.mult, ALU.mult).then_inc(S["s_norm"], 1)

            def cat_low(at, u):
                pool.wait_ge(S["c_hi"], at.ubase + u + 1)
                pool.tensor_tensor(CL[:, u % 2, :], C32[:, u % 2, :], CH[:, u % 2, :], ALU.subtract).then_inc(S["c_lo"], 1)

            def add_x(at, u):
                b = at.graph(u)
                pool.wait_ge(S["lr"], b + 1)
                pool.tensor_tensor(G2.rearrange("p i (b f) -> p b i f", b=B)[:, b], LR, of_graph(at, u), ALU.add)\
                    .then_inc(S["r1"], 1)

            attention(pool, [(norm, "norm"), (negate, "negate")],
                      [(values_high, "values_high"), (values_low, "values_low"), (cat_low, "cat_low")],
                      [(add_x, "add_x")])

            whole_rows(1)
            for s, bias, projected in ((2, bias2, 2 * PAIRS), (3, bias3, 3 * PAIRS)):
                pool.wait_ge(S["ld_b"], LD_B)
                pool.wait_ge(S["f_done"], projected)
                for i in range(NB):
                    pool.tensor_tensor(groups(XB[:, i, :]), groups(XB[:, i, :]),
                                       bias[:, :].unsqueeze(1).broadcast_to([P, B, F]), ALU.add).then_inc(S["xb"], 1)
                whole_rows(s)

        @block.scalar
        def _(act):
            for j in range(NB):
                act.wait_ge(S["at_ps"], j + 1)
                act.activation(ATh[:, j, :], PS[:, j, :], ACT.Copy).then_inc(S["at_hi"], 1)
            for q in range(2):
                act.wait_ge(S["wt_ps"], q + 1)
                act.activation(WT[:, 4 * q:4 * q + 4, :], blocks(4 + q), ACT.Copy).then_inc(S["wt_sb"], 1)
            for q in range(2):
                act.wait_ge(S["g_ps"], q + 1)
                act.activation(GS[:, 4 * q:4 * q + 4, :], blocks(6 + q), ACT.Copy, scale=S_SCALE).then_inc(S["g_hi"], 1)

            def take_xt(s, p):
                n = PAIRS * s + p
                act.wait_ge(S["xt_ps"], n + 1)
                wait(act, "proj_ps", n - 1)
                act.activation(XT[:, n % 2, :], PS[:, 2 + n % 2, :], ACT.Copy).then_inc(S["xt_sb"], 1)

            def p_stage(s, taken=0):
                for p in range(taken, 1):
                    take_xt(s, p)
                for p in range(PAIRS):
                    n = PAIRS * s + p
                    if taken <= p + 1 < PAIRS:
                        take_xt(s, p + 1)
                    act.wait_ge(S["proj_ps"], n + 1)
                    act.activation(Qh[:, QSET[A_OF_P[s]], :, cols(p)], blocks(4 + n % 2), ACT.Copy).then_inc(S["q_hi"], 1)

            def spread(ln, before, between=None):
                for k in range(LN_PIECES + 1):
                    if k < NB:
                        before(k)
                    if k == WHOLE + 1 and between:
                        between()
                    if k:
                        n = LN_PIECES * ln + k - 1
                        if k <= WHOLE:
                            act.wait_ge(S["cen"], WHOLE * ln + k)
                        else:
                            act.wait_ge(S["half_cen"], HALVES * ln + k - WHOLE)
                        act.activation(piece(SQ, ln, k - 1), piece(CEN, ln, k - 1), ACT.Square).then_inc(S["sq"], 1)
                        act.wait_ge(S["var_eps"], n + 1)
                        act.activation(st(ln, k - 1, 4), st(ln, k - 1, 3), ACT.Sqrt).then_inc(S["sd"], 1)

            p_stage(0)
            for i in range(NB):
                for c in (0, 1):
                    act.wait_ge(S["am_ps"], 2 * i + c + 1)
                    act.activation(Z[:, i, halfc(c)], PS[:, c, :], ACT.Relu, scale=1.0 / Q_SCALE).then_inc(S["am_ev"], 1)
            p_stage(1)

            def relu_out(i):
                wait(act, "r_ready", i - 1)
                for c in (0, 1):
                    act.wait_ge(S["am_ps"], 8 + 2 * i + c + 1)
                    act.activation(EV[:, i % 2, halfc(c)], PS[:, c, :], ACT.Relu, scale=1.0 / Q_SCALE).then_inc(S["am_ev"], 1)

            spread(0, relu_out)

            act.wait_ge(S["ld_b"], LD_B)
            act.activation(bhS[:, :], bhT[:, :], ACT.Copy, scale=SLOPE * P_SCALE).then_inc(S["bhs"], 1)
            act.activation(bhP[:, :], bhT[:, :], ACT.Copy, scale=P_SCALE).then_inc(S["bhs"], 1)
            act.wait_ge(S["bhs"], 2)
            act.wait_ge(S["x_rows"], WHOLE)
            act.wait_ge(S["x_halves"], 1)

            def twice(at, u):
                if u % H == 0:
                    b = at.graph(u)
                    wait(act, "pt_ps", b)
                    act.activation(XD, X[:, :, :].rearrange("p i (b f) -> p b i f", b=B)[:, b].unsqueeze(2)
                                   .broadcast_to([P, NB, 2, F]), ACT.Copy).then_inc(S["xd"], 1)

            def columns_high(at, u):
                if u % H == 0:
                    b = at.graph(u)
                    wait(act, "pt_ps", b + 1)
                    act.activation(XHH[:, b, :], bO, ACT.Copy).then_inc(S["xhh"], 1)

            def exps(at, l):
                k = at.base + l
                wait_at_ends(act, "t_ps", k - P_RING + 1)
                wait_at_ends(act, "s_rec", k - V_RING + 1)
                wait(act, "s_neg", k + 1)
                r = l % V_RING
                act.activation(PR[:, l % P_RING, :], TS[:, l % T_RING, :], ACT.Exp, bias=negm[:, r:r + 1],
                               accum_out=rsum[:, r:r + 1]).then_inc(S["s_exp"], 1)

            def probs_high(at, l):
                k = at.base + l
                u, i = l // NB, l % NB
                wait_at_ends(act, "av_ps", at.ubase + u - 1)
                wait(act, "t_ps", k + 1)
                act.activation(PH[:, u % 2, :, P * i:P * i + P], blocks(2 + l % 2), ACT.Copy).then_inc(S["p_hi"], 1)

            def left_high(at, u):
                g = at.ubase + u
                wait_at_ends(act, "s_ps", at.base + NB * (u - 1))
                wait(act, "y_ps", g + 1)
                act.activation(YS[:, u % 2, :], bY, ACT.Copy).then_inc(S["y_hi"], 1)

            def u_high(at, u):
                g = at.ubase + u
                wait_at_ends(act, "o_ps", g - 1)
                wait(act, "av_ps", g + 1)
                act.activation(UA[:, u % 2, :], bU, ACT.Copy).then_inc(S["u_hi"], 1)

            def cat_small(at, u):
                g = at.ubase + u
                h = u % H
                wait_at_ends(act, "c_sb", g)
                wait(act, "o_ps", g + 1)
                act.activation(CS, bO, ACT.Identity, bias=bhS[:, h:h + 1], scale=SLOPE).then_inc(S["c_small"], 1)

            def cat_high(at, u):
                g = at.ubase + u
                wait_at_ends(act, "h2_ps", g - 1)
                wait(act, "c_sb", g + 1)
                act.activation(CH[:, u % 2, :], C32[:, u % 2, :], ACT.Copy).then_inc(S["c_hi"], 1)

            def keep_high(at, u):
                if u % H == H - 1:
                    b = at.graph(u)
                    wait(act, "h2_ps", at.ubase + u + 1)
                    act.activation(H2h[:, b, :], bH, ACT.Copy, scale=H_SCALE / P_SCALE).then_inc(S["h2_hi"], 1)

            def h2_high(at, u):
                b = at.graph(u)
                wait_at_ends(act, "s_ps", at.base + NB * (u - 1))
                wait(act, "pm_cols", b + 1)
                act.activation(XHH2[:, u % 2, :], bY, ACT.Copy).then_inc(S["xh2"], 1)

            def h2_left_high(at, u):
                wait(act, "xh2", at.graph(u) + 1)
                act.activation(YS[0:F, u % 2, :], XHH2[0:F, u % 2, :], ACT.Copy).then_inc(S["y_hi"], 1)

            def h2_rows_high(at, u):
                b = at.graph(u)
                wait_at_ends(act, "av_ps", H * b + H)
                wait(act, "pm_rows", b + 1)
                act.activation(XV[:, b, :, 0:F], blocks(7)[:, :, 0:F], ACT.Copy).then_inc(S["xv2h"], 1)

            def take_u(at, u):
                wait_at_ends(act, "no_ps", at.graph(u) - 1)
                wait(act, "av_ps", at.ubase + u + 1)
                act.activation(US[:, u % 2, :], bU, ACT.Copy).then_inc(S["us_sb"], 1)

            attention(act, [(probs_high, "probs_high"), (exps, "exps")],
                      [(twice, "twice"), (columns_high, "columns_high"), (left_high, "left_high"), (u_high, "u_high"),
                       (cat_small, "cat_small"), (cat_high, "cat_high"), (keep_high, "keep_high")],
                      [(h2_high, "h2_high"), (h2_left_high, "h2_left_high"), (h2_rows_high, "h2_rows_high"),
                       (take_u, "take_u")])

            def take_two():
                take_xt(2, 0)
                take_xt(2, 1)

            spread(1, lambda i: None, take_two)
            p_stage(2, 2)
            for i in range(NB):
                act.wait_ge(S["am_ev"], 16 + 2 * i + 2)
                act.activation(Qh[:, 1, i, :], F1[:, i, :], ACT.Copy, scale=Q_SCALE).then_inc(S["q1_hi"], 1)
            spread(2, lambda i: None)
            p_stage(3)
            spread(3, lambda i: None)

        @block.vector
        def _(dve):
            dve.wait_ge(S["ld_adj"], 16)
            dve.tensor_scalar(MASK[:, :, :], ADJ, 0.0, NEG * S_SCALE, ALU.is_equal, ALU.mult).then_inc(S["adjx"], 1)
            dve.scalar_tensor_tensor(ADJX[:, :, :], ADJ, 0.0, ADJ, ALU.is_equal, ALU.add).then_inc(S["adjx"], 1)
            dve.wait_ge(S["adjx"], 2)
            dve.tensor_scalar(ADJX[:, :, :], ADJX[:, :, :], 1.0 / S_SCALE, None, ALU.mult).then_inc(S["adjx"], 1)
            for j in range(NB):
                dve.wait_ge(S["at_hi"], j + 1)
                dve.tensor_tensor(ATl[:, j, :], PS[:, j, :], ATh[:, j, :], ALU.subtract).then_inc(S["at_lo"], 1)
            dve.wait_ge(S["ld_w"], LD_W)
            dve.wait_ge(S["zeroed"], 3)
            dve.tensor_tensor(tmpw[:, 0, :], WRAW[:, 4, :], WRAW[:, 6, :], ALU.add).then_inc(S["bd_sum"], 1)
            dve.tensor_tensor(tmpw[:, 1, :], WRAW[:, 3, :], WRAW[:, 5, :], ALU.add).then_inc(S["bd_sum"], 1)
            dve.wait_ge(S["bd_sum"], 2)
            for half in (0, 1):
                r = slice(F * half, F * half + F)
                for k, src, scale in ((0, WRAW[r, 0, :], Q_SCALE), (1, WRAW[r, 1, :], Q_SCALE),
                                      (2, tmpw[r, 0, :], 2.0 * Q_SCALE), (3, tmpw[r, 1, :], 1.0),
                                      (5, WRAW[r, 7, :], 1.0), (6, WRAW[r, 8, :], Q_SCALE)):
                    dve.tensor_scalar(BD[r, k, r], src, scale, None, ALU.mult).then_inc(S["bd_ready"], 1)
                dve.tensor_tensor(BD[r, 4, r], WRAW[r, 2, :], tmpw[r, 0, :], ALU.subtract).then_inc(S["bd_ready"], 1)
            for q in range(2):
                dve.wait_ge(S["g_hi"], q + 1)
                dve.scalar_tensor_tensor(GS[F:P, 4 * q:4 * q + 4, :], blocks(6 + q)[F:P], S_SCALE,
                                         GS[F:P, 4 * q:4 * q + 4, :], ALU.mult, ALU.subtract).then_inc(S["g_lo"], 1)

            def p_stage(s):
                for p in range(PAIRS):
                    n = PAIRS * s + p
                    dve.wait_ge(S["proj_ps"], n + 1)
                    if s == 2:
                        dve.tensor_copy(F1[:, :, cols(p)], blocks(FB[0][n % 2])).then_inc(S["f_done"], 1)
                    if s >= 2:
                        dve.tensor_tensor(XB[:, :, cols(p)], blocks(FB[len(PROJ[s]) - 2][n % 2]),
                                          X[:, :, cols(p)], ALU.add).then_inc(S["f_done"], 1)
                    dve.wait_ge(S["q_hi"], n + 1)
                    a = QSET[A_OF_P[s]]
                    dve.tensor_tensor(Ql[:, a, :, cols(p)], blocks(4 + n % 2), Qh[:, a, :, cols(p)],
                                      ALU.subtract).then_inc(S["q_done"], 1)

            def norm_rows(ln, before):
                for k in range(LN_PIECES + 1):
                    if k < LN_PIECES:
                        n = LN_PIECES * ln + k
                        before(k)
                        dve.reduce_sum(st(ln, k, 0), summed(ln, k), AX).then_inc(S["mean_sum"], 1)
                        if k >= WHOLE:
                            dve.wait_ge(S["mean_sum"], n + 1)
                            dve.tensor_scalar(st(ln, k, 1), st(ln, k, 0), -1.0 / F, None, ALU.mult).then_inc(S["half_neg"], 1)
                            dve.wait_ge(S["half_neg"], HALVES * ln + k - WHOLE + 1)
                            dve.tensor_tensor(piece(CEN, ln, k), summed(ln, k), over_features(st(ln, k, 1)), ALU.add)\
                                .then_inc(S["half_cen"], 1)
                    if k:
                        n = LN_PIECES * ln + k - 1
                        q = k - 1
                        dve.wait_ge(S["sq"], n + 1)
                        dve.reduce_sum(st(ln, q, 2), piece(SQ, ln, q), AX).then_inc(S["var_sum"], 1)
                        dve.wait_ge(S["var_sum"], n + 1)
                        dve.tensor_scalar(st(ln, q, 3), st(ln, q, 2), 1.0 / F, EPS, ALU.mult, ALU.add).then_inc(S["var_eps"], 1)
                        dve.wait_ge(S["sd"], n + 1)
                        if q < WHOLE:
                            dve.reciprocal(st(ln, q, 5), st(ln, q, 4)).then_inc(S["rs"], 1)
                            continue
                        n = HALVES * ln + q - WHOLE
                        dve.reciprocal(st(ln, q, 5), st(ln, q, 4)).then_inc(S["half_newton"], 1)
                        dve.wait_ge(S["half_newton"], 4 * n + 1)
                        dve.tensor_tensor(st(ln, q, 6), st(ln, q, 5), st(ln, q, 5), ALU.mult).then_inc(S["half_newton"], 1)
                        dve.wait_ge(S["half_newton"], 4 * n + 2)
                        dve.scalar_tensor_tensor(st(ln, q, 6), st(ln, q, 6), -0.5, st(ln, q, 3), ALU.mult, ALU.mult)\
                            .then_inc(S["half_newton"], 1)
                        dve.wait_ge(S["half_newton"], 4 * n + 3)
                        dve.scalar_tensor_tensor(st(ln, q, 7), st(ln, q, 6), 1.5, st(ln, q, 5), ALU.add, ALU.mult)\
                            .then_inc(S["half_newton"], 1)
                        dve.wait_ge(S["half_newton"], 4 * n + 4)
                        dve.tensor_tensor(piece(X, ln, q), piece(CEN, ln, q), over_features(st(ln, q, 7)),
                                          ALU.mult).then_inc(S["x_halves"], 1)

            p_stage(0)
            p_stage(1)

            def halves(k):
                _first, _end, low, high = PIECES[k]
                return range(low * F // HALF, high * F // HALF)

            def l0_sum(k):
                i = PIECES[k][0]
                both = slice(halves(k)[0] * HALF, (halves(k)[-1] + 1) * HALF)
                dve.wait_ge(S["am_ev"], 8 + 2 * i + halves(k)[-1] + 1)
                dve.tensor_tensor(R[:, i, both], EV[:, i % 2, both], X[:, i, both], ALU.add).then_inc(S["r_ready"], 1)
                dve.wait_ge(S["r_ready"], k + 1)

            norm_rows(0, l0_sum)

            def columns_low(at, u):
                if u % H == 0:
                    b = at.graph(u)
                    wait(dve, "xhh", b + 1)
                    dve.tensor_tensor(XLL[:, b, :], bO, XHH[:, b, :], ALU.subtract).then_inc(S["xll"], 1)

            def scale_max(at, l):
                k = at.base + l
                wait_at_ends(dve, "s_exp", k - T_RING + 1)
                wait_at_ends(dve, "s_neg", k - V_RING + 1)
                wait_at_ends(dve, "s_ps", k + 1)
                r = l % V_RING
                dve.tensor_tensor_reduce(out=TS[:, l % T_RING, :], in0=bS[l % 2], in1=ADJX[:, l % NB, :],
                                         scale=1.0, scalar=-3.0e38, op0=ALU.mult, op1=ALU.max,
                                         accum_out=mx[:, r:r + 1]).then_inc(S["s_max"], 1)

            def recip(at, l):
                k = at.base + l
                wait_at_ends(dve, "s_norm", k - V_RING + 1)
                wait_at_ends(dve, "s_exp", k + 1)
                ahead = k + RECIP_AHEAD + 1
                wait(dve, "s_ps", min(ahead, TILES) if isinstance(ahead, int) else ahead)
                r = l % V_RING
                dve.reciprocal(rinv[:, r:r + 1], rsum[:, r:r + 1]).then_inc(S["s_rec"], 1)

            def probs_low(at, l):
                u, i = l // NB, l % NB
                wait(dve, "p_hi", at.base + l + 1)
                dve.tensor_tensor(PL[:, u % 2, :, P * i:P * i + P], blocks(2 + l % 2),
                                  PH[:, u % 2, :, P * i:P * i + P], ALU.subtract).then_inc(S["p_lo"], 1)

            def left_low(at, u):
                wait(dve, "y_hi", at.ubase + u + 1)
                dve.tensor_tensor(YS[F:P, u % 2, :], bY[F:P], YS[F:P, u % 2, :], ALU.subtract).then_inc(S["y_lo"], 1)

            def u_low(at, u):
                g = at.ubase + u
                wait_at_ends(dve, "o_ps", g - 1)
                wait(dve, "u_hi", g + 1)
                dve.tensor_tensor(UB[0:F, u % 2, :], bU[0:F], UA[0:F, u % 2, :], ALU.subtract).then_inc(S["u_lo"], 1)
                dve.tensor_copy(UB[F:P, u % 2, :], UA[0:F, u % 2, :]).then_inc(S["u_sb"], 1)

            def keep_low(at, u):
                if u % H == H - 1:
                    b = at.graph(u)
                    wait(dve, "h2_hi", b + 1)
                    dve.scalar_tensor_tensor(H2l[:, b, :], bH, H_SCALE / P_SCALE, H2h[:, b, :],
                                             ALU.mult, ALU.subtract).then_inc(S["h2_sb"], 1)

            def cat(at, u):
                g = at.ubase + u
                h = u % H
                wait_at_ends(dve, "c_lo", g - 1)
                wait(dve, "c_small", g + 1)
                dve.scalar_tensor_tensor(C32[:, u % 2, :], bO, bhP[:, h:h + 1], CS, ALU.add, ALU.max).then_inc(S["c_sb"], 1)

            def h2_low(at, u):
                wait(dve, "xh2", at.graph(u) + 1)
                dve.tensor_tensor(XLL2[:, u % 2, :], bY, XHH2[:, u % 2, :], ALU.subtract).then_inc(S["xl2"], 1)

            def h2_left_low(at, u):
                wait(dve, "xl2", at.graph(u) + 1)
                dve.tensor_copy(YS[F:P, u % 2, :], XLL2[F:P, u % 2, :]).then_inc(S["y_lo"], 1)

            def h2_rows_low(at, u):
                b = at.graph(u)
                wait(dve, "xv2h", b + 1)
                dve.tensor_tensor(XV[:, b, :, F:P], blocks(7)[:, :, F:P], XV[:, b, :, 0:F],
                                  ALU.subtract).then_inc(S["xv2l"], 1)

            def take_out(at, u):
                b = at.graph(u)
                wait(dve, "no_ps", b + 1)
                dve.tensor_tensor(G2.rearrange("p i (b f) -> p b i f", b=B)[:, b],
                                  bO[:, 0:NB * F].rearrange("p (i f) -> p i f", i=NB),
                                  bout[:, :].unsqueeze(1).broadcast_to([P, NB, F]), ALU.add).then_inc(S["g2"], 1)

            def leaky(at, u):
                b = at.graph(u)
                if isinstance(b, int) and b == 0:
                    dve.wait_ge(S["pt_ps"], B)
                wait(dve, "r1", b)
                wait(dve, "g2", b + 1)
                g = G2.rearrange("p i (b f) -> p b i f", b=B)[:, b]
                dve.scalar_tensor_tensor(LR, g, SLOPE, g, ALU.mult, ALU.max).then_inc(S["lr"], 1)

            attention(dve, [(scale_max, "scale_max"), (recip, "recip"), (probs_low, "probs_low")],
                      [(columns_low, "columns_low"), (left_low, "left_low"), (u_low, "u_low"), (cat, "cat"),
                       (keep_low, "keep_low")],
                      [(h2_low, "h2_low"), (h2_left_low, "h2_left_low"), (h2_rows_low, "h2_rows_low"),
                       (take_out, "take_out"), (leaky, "leaky")])

            norm_rows(1, lambda k: dve.wait_ge(S["r1"], HB if k < 2 else B))
            p_stage(2)
            for i in range(NB):
                for c in (0, 1):
                    dve.wait_ge(S["am_ps"], 16 + 2 * i + c + 1)
                    dve.scalar_tensor_tensor(F1[:, i, halfc(c)], PS[:, c, :], 1.0 / Q_SCALE, F1[:, i, halfc(c)],
                                             ALU.mult, ALU.add).then_inc(S["am_ev"], 1)
                if i:
                    dve.wait_ge(S["q1_hi"], i)
                    dve.scalar_tensor_tensor(Ql[:, 1, i - 1, :], F1[:, i - 1, :], Q_SCALE, Qh[:, 1, i - 1, :],
                                             ALU.mult, ALU.subtract).then_inc(S["q1_lo"], 1)
            dve.wait_ge(S["q1_hi"], NB)
            dve.scalar_tensor_tensor(Ql[:, 1, NB - 1, :], F1[:, NB - 1, :], Q_SCALE, Qh[:, 1, NB - 1, :],
                                     ALU.mult, ALU.subtract).then_inc(S["q1_lo"], 1)

            def sum_of(a, s):
                def sum_rows(k):
                    i = PIECES[k][0]
                    dve.wait_ge(S["xb"], NB * (s - 2) + i + 1)
                    for c in halves(k):
                        dve.wait_ge(S["am_ps"], 8 * a + 2 * i + c + 1)
                        dve.scalar_tensor_tensor(R[:, i, halfc(c)], PS[:, c, :], 1.0 / Q_SCALE,
                                                 XB[:, i, halfc(c)], ALU.mult, ALU.add).then_inc(S["am_ev"], 1)
                    dve.wait_ge(S["am_ev"], 8 * a + 2 * i + halves(k)[-1] + 1)
                return sum_rows

            norm_rows(2, sum_of(3, 2))
            p_stage(3)
            norm_rows(3, sum_of(4, 3))

        @block.tensor
        def _(pe):
            pe.wait_ge(S["ld_adj"], 16)
            pe.wait_ge(S["consts"], 8)
            for j in range(NB):
                for i in range(NB):
                    last = pe.transpose(PS[:, j, P * i:P * i + P], ADJ[:, i, P * j:P * j + P], ident[:, :])
                last.then_inc(S["at_ps"], 1)
            pe.wait_ge(S["ld_w"], LD_W)
            for q in range(2):
                for k in range(4):
                    last = pe.transpose(blocks(4 + q)[:, k, :], WH2[:, 4 * q + k, :], ident[:, :])
                last.then_inc(S["wt_ps"], 1)
            for q in range(2):
                pe.wait_ge(S["wt_sb"], q + 1)
                for k in range(4):
                    last = pe.matmul(blocks(6 + q)[:, k, :], WT[:, 4 * q + k, :], WT[:, 4 * q + k, :],
                                     start=True, stop=True)
                last.then_inc(S["g_ps"], 1)
            pe.wait_ge(S["at_lo"], NB)
            pe.wait_ge(S["wt_sb"], 2)
            pe.wait_ge(S["bd_ready"], 14)

            def p_stage(s):
                src = Z if s == 1 else X

                def turn(p):
                    n = PAIRS * s + p
                    wait(pe, "xt_sb", n - 1)
                    if s == 0 and p % (PAIRS // 2) == 0:
                        pe.wait_ge(S["ld_x2" if p else "ld_x"], 16 * NB)
                    if s == 2 and p == 0:
                        normed(pe, 1, 1)
                    if s == 2 and p == PAIRS // 2:
                        normed(pe, 1, WHOLE - 1)
                        normed(pe, 1, LN_PIECES - 1)
                    if s == 3 and p == 0:
                        normed(pe, 2, WHOLE - 1)
                    if s == 3 and p % (PAIRS // HALVES) == 0:
                        normed(pe, 2, WHOLE + p // (PAIRS // HALVES))
                    for i in range(NB):
                        last = pe.transpose(blocks(2 + n % 2)[:, i, :], src[:, i, cols(p)], ident[:, :])
                    last.then_inc(S["xt_ps"], 1)

                turn(0)
                for p in range(PAIRS):
                    n = PAIRS * s + p
                    if p + 1 < PAIRS:
                        turn(p + 1)
                    pe.wait_ge(S["xt_sb"], n + 1)
                    wait(pe, "q_done", n - 1)
                    for k, w in enumerate(PROJ[s]):
                        bank = 4 + n % 2 if k == 0 else FB[k - 1][n % 2]
                        for i in range(NB):
                            last = pe.matmul(blocks(bank)[:, i, :], XT[:, n % 2, P * i:P * i + P], BD[:, w, :],
                                             start=True, stop=True)
                    last.then_inc(S["proj_ps"], 1)

            def a_stage(a, ready):
                q = QSET[a]

                def rows(i, m, first):
                    for c in (0, 1):
                        if not first:
                            pe.wait_ge(S["am_ev"], m + c - 1)
                        for k in range(3 * NB):
                            j, way = k // 3, k % 3
                            if way == 0 and isinstance(i, int):
                                ready(c, j)
                            left = ATl if way == 2 else ATh
                            right = Ql if way == 1 else Qh
                            last = pe.matmul(PS[:, c, :], left[:, j, bass.ds(P * i, P)], right[:, q, j, halfc(c)],
                                             start=(k == 0), stop=(k == 3 * NB - 1))
                        last.then_inc(S["am_ps"], 1)

                rows(0, 8 * a, a == 0)
                with pe.Fori(1, NB) as i:
                    rows(i, 8 * a + 2 * i, False)

            def keep_clock(count):
                with pe.Fori(0, count // 4):
                    for _ in range(4):
                        pe.matmul(PS[:, 4, :], identb[:, :], MASK[:, 0, :], start=True, stop=True)

            def projected(s):
                def ready(c, j):
                    if j == 0:
                        pairs = PAIRS if c else PAIRS - 1 if s == 2 else PAIRS // 2
                        pe.wait_ge(S["q_done"], PAIRS * s + pairs)
                return ready

            p_stage(0)
            a_stage(0, projected(0))
            pe.wait_ge(S["am_ev"], 8)
            p_stage(1)
            a_stage(1, projected(1))

            pe.wait_ge(S["g_lo"], 2)
            pe.wait_ge(S["wo"], 2)
            pe.wait_ge(S["wd"], 3)
            pe.wait_ge(S["adjx"], 3)
            keep_clock(44)

            def columns(at, u):
                if u % H == 0:
                    b = at.graph(u)
                    wait(pe, "c_sb", at.ubase + u - 5)
                    wait(pe, "xd", b + 1)
                    for i in range(NB):
                        last = pe.transpose(blocks(5)[:, i, :], XD[:, i].rearrange("p t f -> p (t f)"), ident[:, :])
                    last.then_inc(S["pt_ps"], 1)

            def scores(at, l):
                k = at.base + l
                u, i = l // NB, l % NB
                if at.heads:
                    if i == 0:
                        wait(pe, "y_lo", at.ubase + u + 1)
                    hi, lo = XHH[:, at.graph(u), :], XLL[:, at.graph(u), :]
                else:
                    if i == 0:
                        wait(pe, "y_lo", at.ubase + u + 1)
                        wait(pe, "y_hi", at.ubase + u + 1)
                    hi, lo = XHH2[:, u % 2, :], XLL2[:, u % 2, :]
                wait(pe, "s_max", k - 1)
                pe.matmul(bS[l % 2], identb[:, :], MASK[:, i, :], start=True, stop=False)
                pe.matmul(bS[l % 2], YS[:, u % 2, P * i:P * i + P], hi, start=False, stop=False)
                pe.matmul(bS[l % 2], YS[:, u % 2, P * i:P * i + P], lo, start=False, stop=True)\
                    .then_inc(S["s_ps"], 1)

            def turn_probs(at, l):
                k = at.base + l
                wait_at_ends(pe, "p_lo", k - 1)
                wait(pe, "s_norm", k + 1)
                for j in range(NB):
                    last = pe.transpose(blocks(2 + l % 2)[:, j, :], PR[:, l % P_RING, P * j:P * j + P], ident[:, :])
                last.then_inc(S["t_ps"], 1)

            def left_proj(at, u):
                g = at.ubase + u
                wait(pe, "y_lo", g)
                if u % H == 0:
                    wait(pe, "xll", at.graph(u) + 1)
                pe.matmul(bY, GS[:, u % H, :], XHH[:, at.graph(u), :], start=True, stop=False)
                pe.matmul(bY, GS[:, u % H, :], XLL[:, at.graph(u), :], start=False, stop=True).then_inc(S["y_ps"], 1)

            def times_values(at, u):
                g = at.ubase + u
                if at.heads or u == 0:
                    wait_at_ends(pe, "u_sb", min(g, H * B) if isinstance(g, int) else g)
                if not at.heads:
                    wait_at_ends(pe, "us_sb", at.graph(u))
                    wait(pe, "xv2l", at.graph(u) + 1)
                elif u % H == 0:
                    wait(pe, "xvl", at.graph(u) + 1)
                wait(pe, "p_lo", at.base + NB * u + NB)
                for j in range(NB):
                    v = XV[:, at.graph(u), j, :]
                    pe.matmul(bU, v, PH[:, u % 2, j, :], start=(j == 0), stop=False)
                    last = pe.matmul(bU, v, PL[:, u % 2, j, :], start=False, stop=(j == NB - 1))
                last.then_inc(S["av_ps"], 1)

            def head_out(at, u):
                g = at.ubase + u
                wait_at_ends(pe, "c_sb", g)
                if u == -5 and at.it is not B:
                    wait(pe, "xll", at.graph(u) + 2)
                wait(pe, "u_sb", g + 1)
                pe.matmul(bO, Wa[:, u % H, :], UA[:, u % 2, :], start=True, stop=False)
                pe.matmul(bO, Wb[:, u % H, :], UB[:, u % 2, :], start=False, stop=True).then_inc(S["o_ps"], 1)

            def add_h2(at, u):
                h = u % H
                if h == 0:
                    wait(pe, "h2_sb", at.graph(u))
                wait(pe, "c_lo", at.ubase + u + 1)
                pe.matmul(bH, WO[:, h, :], CH[:, u % 2, :], start=(h == 0), stop=False)
                pe.matmul(bH, WO[:, h, :], CL[:, u % 2, :], start=False, stop=(h == H - 1)).then_inc(S["h2_ps"], 1)

            def sum_h2(at, u):
                b = at.graph(u)
                wait_at_ends(pe, "h2_sb", b + 1)
                if isinstance(b, int):
                    wait(pe, "y_lo", H * B)
                wait(pe, "xv2l", b)
                pe.matmul(bY, IIh[:, :], H2h[:, b, :], start=True, stop=False)
                pe.matmul(bY, IIh[:, :], H2l[:, b, :], start=False, stop=True).then_inc(S["pm_cols"], 1)

            def sum_h2_rows(at, u):
                b = at.graph(u)
                wait(pe, "xl2", b + 1)
                for i in range(NB):
                    pe.matmul(blocks(7)[:, i, :], H2h[:, b, P * i:P * i + P], IIh[:, :], start=True, stop=False)
                    last = pe.matmul(blocks(7)[:, i, :], H2l[:, b, P * i:P * i + P], IIh[:, :],
                                     start=False, stop=True)
                last.then_inc(S["pm_rows"], 1)

            def rows_out(at, u):
                b = at.graph(u)
                if isinstance(b, int):
                    wait(pe, "c_sb", H * B)
                wait(pe, "g2", b)
                wait(pe, "us_sb", b + 1)
                for i in range(NB):
                    last = pe.matmul(bO[:, F * i:F * i + F], US[:, u % 2, P * i:P * i + P], IIs[:, :],
                                     start=True, stop=True)
                last.then_inc(S["no_ps"], 1)

            attention(pe, [(scores, "scores"), (turn_probs, "turn_probs")],
                      [(columns, "columns"), (left_proj, "left_proj"), (times_values, "times_values"),
                       (head_out, "head_out"), (add_h2, "add_h2")],
                      [(sum_h2, "sum_h2"), (sum_h2_rows, "sum_h2_rows"), (times_values, "out_values"),
                       (rows_out, "rows_out")])

            keep_clock(68)
            p_stage(2)
            a_stage(2, projected(2))
            a_stage(3, lambda c, j: pe.wait_ge(S["q1_lo"], j + 1) if c == 0 else None)
            keep_clock(32)
            p_stage(3)
            a_stage(4, projected(3))


_INS = ["x", "adj", "L0_gnn_net_params", "L1_gnn_Wh", "L1_gnn_bh", "L1_gnn_W_out", "L1_gnn_b_out",
        "L2_gnn_weight", "L2_gnn_bias", "L3_gnn_weight_self", "L3_gnn_weight_neighbor", "L3_gnn_bias"]


def kernel(**inputs):
    import numpy as _np
    import concourse.bacc as _bacc
    from concourse import mybir as _mybir
    from concourse.bass_utils import run_bass_kernel_spmd as _run

    nc = _bacc.Bacc("TRN2", target_bir_lowering=False, num_devices=1)
    arrays, args = {}, []
    for name in _INS:
        a = _np.ascontiguousarray(inputs[name])
        arrays[f"in_{name}_dram"] = a
        args.append(nc.dram_tensor(f"in_{name}_dram", a.shape, _mybir.dt.from_np(a.dtype), kind="ExternalInput").ap())
    args.append(nc.dram_tensor("out_0_dram", (B, N, F), _mybir.dt.float32, kind="ExternalOutput").ap())
    build(nc, *args)
    r = _run(nc, [arrays], core_ids=[0])
    return r.results[0]["out_0_dram"]
```
